# Optimizing a Trainium2 kernel written in Bass

```python
import numpy as np
import jax
import jax.numpy as jnp

def _softmax(x, axis=-1):
    return jax.nn.softmax(x, axis=axis)

def _gelu(x):
    return jax.nn.gelu(x, approximate=True)

def _silu(x):
    return jax.nn.silu(x)

def _sigmoid(x):
    return jax.nn.sigmoid(x)

def _layernorm(x, axis=-1, eps=1e-05):
    m = jnp.mean(x, axis=axis, keepdims=True)
    v = jnp.var(x, axis=axis, keepdims=True)
    return (x - m) / jnp.sqrt(v + eps)

def _scatter_add(tgt, idx, src, axis=0):
    return tgt.at[idx].add(src)

def _segment_sum(src, seg, n):
    return jax.ops.segment_sum(src, seg, n)
kernel_name = 'mk_macaron_d1_jaxref_r8_000ea0'

def setup_inputs(seed: int=0):
    np.random.seed(seed)
    _w = jnp.asarray

    def _L0_attn_setup():
        import jax, jax.numpy as jnp
        import numpy as np
        N_HEADS = 16

        def _rope_tables(seq_len, head_dim, dtype=jnp.float32):
            pos = jnp.arange(seq_len, dtype=jnp.float32)[:, None]
            exps = -jnp.arange(0, head_dim, 2, dtype=jnp.float32) / head_dim
            thetas = jnp.repeat(jnp.power(10000.0, exps), 2)
            angles = pos * thetas[None, :]
            return (jnp.cos(angles).astype(dtype), jnp.sin(angles).astype(dtype))

        def _apply_rope(x, cos, sin):
            x_even = x[..., 0::2]
            x_odd = x[..., 1::2]
            x_rot = jnp.stack((-x_odd, x_even), axis=-1).reshape(x.shape)
            return x * cos[None, :, None, :] + x_rot * sin[None, :, None, :]
        key = jax.random.key(seed)
        ks = jax.random.split(key, 5)
        B, S, E = (2, 256, 256)
        scale = 1.0 / np.sqrt(E)
        return {'x': jax.random.normal(ks[0], (B, S, E), dtype=jnp.float32), 'Wq': jax.random.normal(ks[1], (E, E), dtype=jnp.float32) * scale, 'bq': jnp.zeros((E,), dtype=jnp.float32), 'Wk': jax.random.normal(ks[2], (E, E), dtype=jnp.float32) * scale, 'bk': jnp.zeros((E,), dtype=jnp.float32), 'Wv': jax.random.normal(ks[3], (E, E), dtype=jnp.float32) * scale, 'bv': jnp.zeros((E,), dtype=jnp.float32), 'Wo': jax.random.normal(ks[4], (E, E), dtype=jnp.float32) * scale, 'bo': jnp.zeros((E,), dtype=jnp.float32)}
    _L0_attn_in = _L0_attn_setup()

    def _L0_ffn_setup():
        import jax, jax.numpy as jnp
        import numpy as np
        B, S, D, H = (4, 256, 256, 1024)

        def fwht(x):
            orig_shape = x.shape
            n = orig_shape[-1]
            x = x.reshape(-1, n)
            h = 1
            while h < n:
                xb = x.reshape(-1, n // (2 * h), 2, h)
                a = xb[:, :, 0, :]
                b = xb[:, :, 1, :]
                x = jnp.stack([a + b, a - b], axis=2).reshape(-1, n)
                h *= 2
            scale = jnp.asarray(1.0 / np.sqrt(n), dtype=x.dtype)
            return (x * scale).reshape(orig_shape)
        key = jax.random.key(seed)
        kx, k1, k2, k3 = jax.random.split(key, 4)
        x = jax.random.normal(kx, (B, S, D), dtype=jnp.float32)
        W1 = jax.random.normal(k1, (H, D), dtype=jnp.float32) * (1.0 / np.sqrt(D))
        W2 = jax.random.normal(k2, (D, H), dtype=jnp.float32) * (1.0 / np.sqrt(H))
        W3 = jax.random.normal(k3, (H, D), dtype=jnp.float32) * (1.0 / np.sqrt(D))
        return {'x': x, 'W1': W1, 'W2': W2, 'W3': W3}
    _L0_ffn_in = _L0_ffn_setup()
    _d = {'L0_attn_x': _L0_attn_in['x'], 'L0_attn_Wq': _L0_attn_in['Wq'], 'L0_attn_bq': _L0_attn_in['bq'], 'L0_attn_Wk': _L0_attn_in['Wk'], 'L0_attn_bk': _L0_attn_in['bk'], 'L0_attn_Wv': _L0_attn_in['Wv'], 'L0_attn_bv': _L0_attn_in['bv'], 'L0_attn_Wo': _L0_attn_in['Wo'], 'L0_attn_bo': _L0_attn_in['bo'], 'L0_ffn_W1': _L0_ffn_in['W1'], 'L0_ffn_W2': _L0_ffn_in['W2'], 'L0_ffn_W3': _L0_ffn_in['W3']}
    _x0 = _d['L0_attn_x']
    _d['L0_attn_x'] = jax.random.normal(jax.random.fold_in(jax.random.key(seed), 1), (4, 1024, 256), dtype=_x0.dtype)
    del _x0
    return _d

def reference(L0_attn_x, L0_attn_Wq, L0_attn_bq, L0_attn_Wk, L0_attn_bk, L0_attn_Wv, L0_attn_bv, L0_attn_Wo, L0_attn_bo, L0_ffn_W1, L0_ffn_W2, L0_ffn_W3):

    def _L0_attn_ref(x, Wq, bq, Wk, bk, Wv, bv, Wo, bo):
        import jax, jax.numpy as jnp
        import numpy as np
        N_HEADS = 16

        def _rope_tables(seq_len, head_dim, dtype=jnp.float32):
            pos = jnp.arange(seq_len, dtype=jnp.float32)[:, None]
            exps = -jnp.arange(0, head_dim, 2, dtype=jnp.float32) / head_dim
            thetas = jnp.repeat(jnp.power(10000.0, exps), 2)
            angles = pos * thetas[None, :]
            return (jnp.cos(angles).astype(dtype), jnp.sin(angles).astype(dtype))

        def _apply_rope(x, cos, sin):
            x_even = x[..., 0::2]
            x_odd = x[..., 1::2]
            x_rot = jnp.stack((-x_odd, x_even), axis=-1).reshape(x.shape)
            return x * cos[None, :, None, :] + x_rot * sin[None, :, None, :]
        B, S, E = x.shape
        H = N_HEADS
        D = E // H
        cos, sin = _rope_tables(S, D, x.dtype)
        q = (x @ Wq + bq).reshape(B, S, H, D)
        k = (x @ Wk + bk).reshape(B, S, H, D)
        v = (x @ Wv + bv).reshape(B, S, H, D)
        q = _apply_rope(q, cos, sin)
        k = _apply_rope(k, cos, sin)
        scores = jnp.einsum('bshd,bthd->bhst', q, k) / jnp.sqrt(jnp.asarray(D, x.dtype))
        causal = jnp.triu(jnp.ones((S, S), dtype=bool), k=1)
        scores = jnp.where(causal[None, None], -jnp.inf, scores)
        attn = jax.nn.softmax(scores, axis=-1)
        out = jnp.einsum('bhst,bthd->bshd', attn, v).reshape(B, S, E)
        return out @ Wo + bo

    def _L0_ffn_ref(x, W1, W2, W3):
        import jax, jax.numpy as jnp
        import numpy as np
        B, S, D, H = (4, 256, 256, 1024)

        def fwht(x):
            orig_shape = x.shape
            n = orig_shape[-1]
            x = x.reshape(-1, n)
            h = 1
            while h < n:
                xb = x.reshape(-1, n // (2 * h), 2, h)
                a = xb[:, :, 0, :]
                b = xb[:, :, 1, :]
                x = jnp.stack([a + b, a - b], axis=2).reshape(-1, n)
                h *= 2
            scale = jnp.asarray(1.0 / np.sqrt(n), dtype=x.dtype)
            return (x * scale).reshape(orig_shape)
        up_gate = jnp.einsum('bsd,hd->bsh', x, W1)
        up_lin = jnp.einsum('bsd,hd->bsh', x, W3)
        hidden = jax.nn.silu(up_gate) * up_lin
        hidden = fwht(hidden)
        out = jnp.einsum('bsh,dh->bsd', hidden, W2)
        return out
    x = L0_attn_x
    x = x + 0.5 * _L0_ffn_ref(_layernorm(x, axis=-1), L0_ffn_W1, L0_ffn_W2, L0_ffn_W3)
    x = x + _L0_attn_ref(_layernorm(x, axis=-1), L0_attn_Wq, L0_attn_bq, L0_attn_Wk, L0_attn_bk, L0_attn_Wv, L0_attn_bv, L0_attn_Wo, L0_attn_bo)
    x = x + 0.5 * _L0_ffn_ref(_layernorm(x, axis=-1), L0_ffn_W1, L0_ffn_W2, L0_ffn_W3)
    return x

_drawn_inputs = setup_inputs


def setup_inputs(seed=0):
    import zlib

    import numpy as np

    out = dict(_drawn_inputs(seed))
    spreads = {'L0_attn_bq': (0.0, 0.799),
     'L0_attn_bk': (0.0, 0.8),
     'L0_attn_bv': (0.0, 0.1),
     'L0_attn_bo': (0.0, 0.1)}
    factors = {}
    for name, (base, spread) in spreads.items():
        noise = np.random.default_rng([zlib.crc32(name.encode()), seed]).standard_normal(out[name].shape)
        drawn = base * np.exp(spread * noise) if base else spread * noise
        out[name] = jnp.asarray(drawn.astype(out[name].dtype))
    for name, factor in factors.items():
        out[name] = (out[name] * factor).astype(out[name].dtype)
    return out
```

```python
from contextlib import ExitStack

import numpy as np

import concourse.bass as bass
from concourse import mybir

F32 = mybir.dt.float32
F32R = mybir.dt.float32r
I32 = mybir.dt.int32
ALU = mybir.AluOpType
ACT = mybir.ActivationFunctionType
AX = mybir.AxisListType

P = 128
B, S, D = 4, 1024, 256
HID = 1024
NH = 16
DH = D // NH
TOK = B * S
CH = 512
NC = TOK // CH
TPC = CH // P
KD = D // P
NHT = HID // P
EPS = 1e-5
QUADS = B * NH // 4
NB = S // P
NEG = -1e38
SCALE = float(DH) ** -0.5


def later(value):
    return not isinstance(value, int) or value > 0


def build_program(nc, x, w1t, w3t, w2t, wqkvo, bqk, bvo, cos_t, sin_t, hadamard, identity, causal, out):
    with ExitStack() as ctx:
        def sb(name, shape, dt=F32, scope=ctx):
            return scope.enter_context(nc.sbuf_tensor(name, shape, dt))

        def sem(name):
            return ctx.enter_context(nc.semaphore(name))

        dve_passed, pool_passed = sem("dve_passed"), sem("pool_passed")

        qk_d = nc.dram_tensor("qk_scratch", [2, 2, NC, D, CH], F32, kind="Internal").ap()
        v_d = nc.dram_tensor("v_scratch", [TOK, NH * 32], F32, kind="Internal").ap()
        x1_d = nc.dram_tensor("x1_scratch", [TOK, D], F32, kind="Internal").ap()
        att_d = nc.dram_tensor("att_scratch", [NC, D, CH], F32, kind="Internal").ap()
        rec_d = nc.dram_tensor("rec_scratch", [QUADS, 4, S], F32, kind="Internal").ap()

        w1_h, w1_l = sb("w1_h", [P, KD, HID], F32R), sb("w1_l", [P, KD, HID], F32R)
        w3_h, w3_l = sb("w3_h", [P, KD, HID], F32R), sb("w3_l", [P, KD, HID], F32R)
        w2_h, w2_l = sb("w2_h", [P, NHT, D], F32R), sb("w2_l", [P, NHT, D], F32R)
        wp_h, wp_l = sb("wp_h", [P, 4, KD, D], F32R), sb("wp_l", [P, 4, KD, D], F32R)
        ident = sb("ident", [P, P])
        bqk_s = sb("bqk_s", [P, 2, KD])
        bvo_s = sb("bvo_s", [P, 2, D])
        ps = ctx.enter_context(nc.psum_tensor("ps", [P, 8, CH], F32))
        GATE, LIN, YB, TB = (0, 1), (2, 3), 4, 6

        raw_loaded, const_loaded = sem("raw_loaded"), sem("const_loaded")
        high_ready, low_ready, fwht_step = sem("high_ready"), sem("low_ready"), sem("fwht_step")
        w2x_h_ready, w2x_ready, had_ready, w2_ps_ready = (
            sem("w2x_h_ready"), sem("w2x_ready"), sem("had_ready"), sem("w2_ps_ready"))
        w2_h_ready, w2_l_ready = sem("w2_h_ready"), sem("w2_l_ready")
        with ExitStack() as scope:
            w1_raw = sb("w1_raw", [P, KD, HID], F32, scope)
            w3_raw = sb("w3_raw", [P, KD, HID], F32, scope)
            wp_raw = sb("wp_raw", [P, 4, KD, D], F32, scope)
            fa = sb("fa", [P, NHT, D], F32, scope)
            fb = sb("fb", [P, NHT, D], F32, scope)
            w2x_h, w2x_l = sb("w2x_h", [P, NHT, D], F32R, scope), sb("w2x_l", [P, NHT, D], F32R, scope)
            had_raw, had = sb("had_raw", [P, P], F32, scope), sb("had", [P, P], F32R, scope)
            with nc.Block() as block:
                @block.sync
                def _(sp):
                    sp.dma_start(fa[:], w2t.rearrange("(c p) d -> p c d", p=P)).then_inc(raw_loaded, 16)
                    sp.dma_start(w1_raw[:], w1t.rearrange("(k p) h -> p k h", p=P)).then_inc(raw_loaded, 16)
                    sp.dma_start(w3_raw[:], w3t.rearrange("(k p) h -> p k h", p=P)).then_inc(raw_loaded, 16)
                    sp.dma_start(wp_raw[:], wqkvo.rearrange("w (k p) e -> p w k e", p=P)).then_inc(raw_loaded, 16)
                    sp.dma_start(had_raw[:], hadamard).then_inc(raw_loaded, 16)
                    sp.dma_start(ident[:], identity).then_inc(const_loaded, 16)
                    sp.dma_start(bqk_s[:], bqk).then_inc(const_loaded, 16)
                    sp.dma_start(bvo_s[:], bvo).then_inc(const_loaded, 16)
                    sp.wait_ge(const_loaded, 48)

                @block.scalar
                def _(act):
                    act.wait_ge(raw_loaded, 80)
                    for high, raw in ((w1_h, w1_raw), (w3_h, w3_raw), (wp_h, wp_raw)):
                        act.activation(high[:], raw[:], ACT.Identity).then_inc(high_ready, 1)
                    act.activation(had[:], had_raw[:], ACT.Identity).then_inc(had_ready, 1)
                    act.wait_ge(fwht_step, 6)
                    act.activation(w2x_h[:], fb[:], ACT.Identity).then_inc(w2x_h_ready, 1)
                    act.wait_ge(w2_ps_ready, NHT)
                    act.activation(w2_h[:], ps[:, 0:4, :].rearrange("p b (c d) -> p (b c) d", d=D), ACT.Identity,
                                   scale=0.5 / 32.0).then_inc(w2_h_ready, 1)

                @block.vector
                def _(dve):
                    dve.wait_ge(raw_loaded, 80)
                    for n, (src, dst, half) in enumerate(((fa, fb, 1), (fb, fa, 2), (fa, fb, 4))):
                        s = src[:].rearrange("p (g two h) d -> p g two (h d)", two=2, h=half)
                        d = dst[:].rearrange("p (g two h) d -> p g two (h d)", two=2, h=half)
                        if n:
                            dve.wait_ge(fwht_step, 2 * n)
                        dve.tensor_tensor(d[:, :, 0], s[:, :, 0], s[:, :, 1], ALU.add).then_inc(fwht_step, 1)
                        dve.tensor_tensor(d[:, :, 1], s[:, :, 0], s[:, :, 1], ALU.subtract).then_inc(fwht_step, 1)
                    dve.wait_ge(w2x_h_ready, 1)
                    dve.tensor_tensor(w2x_l[:], fb[:], w2x_h[:].bitcast(F32), ALU.subtract).then_inc(w2x_ready, 1)
                    for n, (low, high, raw) in enumerate(((w1_l, w1_h, w1_raw), (w3_l, w3_h, w3_raw), (wp_l, wp_h, wp_raw))):
                        dve.wait_ge(high_ready, n + 1)
                        dve.tensor_tensor(low[:], raw[:], high[:].bitcast(F32), ALU.subtract).then_inc(low_ready, 1)
                    dve.wait_ge(w2_h_ready, 1)
                    dve.scalar_tensor_tensor(w2_l[:].rearrange("p c d -> p (c d)"),
                                             ps[:, 0:4, :].rearrange("p b n -> p (b n)"), 0.5 / 32.0,
                                             w2_h[:].bitcast(F32).rearrange("p c d -> p (c d)"),
                                             ALU.mult, ALU.subtract).then_inc(w2_l_ready, 1)

                @block.tensor
                def _(pe):
                    pe.wait_ge(had_ready, 1)
                    pe.wait_ge(w2x_ready, 1)
                    for c in range(NHT):
                        dst = ps[:, c // 2, (c % 2) * D:(c % 2 + 1) * D]
                        pe.matmul(dst, had[:], w2x_h[:, c, :], start=True, stop=False)
                        pe.matmul(dst, had[:], w2x_l[:, c, :], start=False, stop=True).then_inc(w2_ps_ready, 1)

        xin_loaded, xres_ready = sem("xin_loaded"), sem("xres_ready")
        stats_ready, var_ready, rstd_ready, xn_ready = sem("stats_ready"), sem("var_ready"), sem("rstd_ready"), sem("xn_ready")
        seed_ready, newton_step = sem("seed_ready"), sem("newton_step")
        xT_ready, xh_ready, xl_ready = sem("xT_ready"), sem("xh_ready"), sem("xl_ready")
        gate_ready, lin_ready, silu_ready, hid_ready = sem("gate_ready"), sem("lin_ready"), sem("silu_ready"), sem("hid_ready")
        hh_ready, hl_ready, y_ready, xo_ready, xo_stored = (
            sem("hh_ready"), sem("hl_ready"), sem("y_ready"), sem("xo_ready"), sem("xo_stored"))

        class Buffers:
            pass

        def ffn_buffers(scope, t):
            f = Buffers()
            f.xin = sb(f"xin{t}", [P, TPC, D], F32, scope)
            f.xres = sb(f"xres{t}", [P, TPC, D], F32, scope)
            f.xn = sb(f"xn{t}", [P, TPC, D], F32, scope)
            f.xh = sb(f"xh{t}", [P, KD, CH], F32R, scope)
            f.xl = sb(f"xl{t}", [P, KD, CH], F32R, scope)
            f.silu = sb(f"silu{t}", [P, 2, CH], F32, scope)
            f.hid = sb(f"hid{t}", [P, 2, CH], F32, scope)
            f.hh = sb(f"hh{t}", [P, NHT, CH], F32R, scope)
            f.hl = sb(f"hl{t}", [P, NHT, CH], F32R, scope)
            f.xo = sb(f"xo{t}", [P, TPC, D], F32, scope)
            f.stats = sb(f"stats{t}", [P, TPC, 6], F32, scope)
            f.mv = sb(f"mv{t}", [P, TPC, 2], F32, scope)
            f.rstd = sb(f"rstd{t}", [P, TPC], F32, scope)
            f.veps, f.newt = sb(f"veps{t}", [P, TPC], F32, scope), sb(f"newt{t}", [P, TPC], F32, scope)
            f.bits = sb(f"bits{t}", [P, TPC], I32, scope)
            return f

        def ln_stats(dve, src, f, n, stats_done, var_done, seed_done):
            for j in range(TPC):
                dve.bn_stats(f.stats[:, j, :], src[:, j, :]).then_inc(stats_done, 1)
            for j in range(TPC):
                dve.wait_ge(stats_done, TPC * n + j + 1)
                dve.sem_inc(dve_passed)
                dve.bn_aggr(f.mv[:, j, :], f.stats[:, j, :]).then_inc(var_done, 1)
            dve.wait_ge(var_done, TPC * n + TPC)
            dve.tensor_scalar(f.veps[:], f.mv[:, :, 1], EPS, None, ALU.add).then_inc(seed_done, 1)
            dve.wait_ge(seed_done, 3 * n + 1)
            dve.tensor_scalar(f.bits[:], f.veps[:].bitcast(I32), 1, None, ALU.logical_shift_right).then_inc(seed_done, 1)
            dve.wait_ge(seed_done, 3 * n + 2)
            dve.tensor_scalar(f.rstd[:].bitcast(I32), f.bits[:], -1.0, float(0x5F3759DF), ALU.mult, ALU.add)\
               .then_inc(seed_done, 1)

        def ln_rstd(pool, f, n, seed_done, newton_done, rstd_done):
            pool.wait_ge(seed_done, 3 * n + 3)
            done = 11 * n
            for step in range(3):
                last = step == 2
                if step:
                    pool.wait_ge(newton_done, done)
                pool.tensor_tensor(f.newt[:], f.rstd[:], f.rstd[:], ALU.mult).then_inc(newton_done, 1)
                pool.wait_ge(newton_done, done + 1)
                pool.tensor_tensor(f.newt[:], f.newt[:], f.veps[:], ALU.mult).then_inc(newton_done, 1)
                pool.wait_ge(newton_done, done + 2)
                pool.sem_inc(pool_passed)
                pool.tensor_scalar(f.newt[:], f.newt[:], -0.5, 1.5, ALU.mult, ALU.add).then_inc(newton_done, 1)
                pool.wait_ge(newton_done, done + 3)
                pool.tensor_tensor(f.rstd[:], f.rstd[:], f.newt[:], ALU.mult).then_inc(rstd_done if last else newton_done, 1)
                done = done + 4

        def ln_scale(dve, dst, src, f, n, rstd_done, done):
            dve.wait_ge(rstd_done, n + 1)
            for j in range(TPC):
                ins = dve.tensor_scalar(dst[:, j, :], src[:, j, :], f.mv[:, j, 0:1], f.rstd[:, j:j + 1],
                                        ALU.subtract, ALU.mult)
            ins.then_inc(done, 1)

        def pe_transpose(pe, src, done):
            for k in range(KD):
                for j in range(TPC):
                    ins = pe.transpose(ps[:, TB + k, j * P:(j + 1) * P], src[:, j, k * P:(k + 1) * P], ident[:])
                ins.then_inc(done, 1)

        def pe_up(pe, f, n, hts, banks_free=None):
            for ht in hts:
                g, r = n * NHT + ht, ht % 2
                if ht == 0:
                    pe.wait_ge(xh_ready, KD * n + KD)
                    pe.wait_ge(xl_ready, KD * n + KD)
                    if banks_free is not None and later(banks_free[1]):
                        pe.wait_ge(*banks_free)
                for w_h, w_l, bank, freed, done in ((w1_h, w1_l, GATE[r], silu_ready, gate_ready),
                                                    (w3_h, w3_l, LIN[r], hid_ready, lin_ready)):
                    if later(g - 1):
                        pe.wait_ge(freed, g - 1)
                    cols = slice(ht * P, (ht + 1) * P)
                    for k in range(KD):
                        pe.matmul(ps[:, bank, :], w_h[:, k, cols], f.xh[:, k, :], start=(k == 0), stop=False)
                        pe.matmul(ps[:, bank, :], w_h[:, k, cols], f.xl[:, k, :], start=False, stop=False)
                        ins = pe.matmul(ps[:, bank, :], w_l[:, k, cols], f.xh[:, k, :], start=False, stop=(k == KD - 1))
                    ins.then_inc(done, 1)

        def pe_down(pe, f, n, tiles):
            for j in tiles:
                dst = ps[:, YB + j // 2, (j % 2) * D:(j % 2 + 1) * D]
                if j % 2 == 0 and later(2 * n - 1 + j // 2):
                    pe.wait_ge(xo_ready, 2 * n - 1 + j // 2)
                for ht in range(NHT):
                    if j == 0:
                        pe.wait_ge(hh_ready, NHT * n + ht + 1)
                        pe.wait_ge(hl_ready, NHT * n + ht + 1)
                    cols = slice(j * P, (j + 1) * P)
                    pe.matmul(dst, f.hh[:, ht, cols], w2_h[:, ht, :], start=(ht == 0), stop=False)
                    pe.matmul(dst, f.hh[:, ht, cols], w2_l[:, ht, :], start=False, stop=False)
                    ins = pe.matmul(dst, f.hl[:, ht, cols], w2_h[:, ht, :], start=False, stop=(ht == NHT - 1))
                ins.then_inc(y_ready, 1)

        def act_x_high(act, dst, n, transposed, done):
            for k in range(KD):
                act.wait_ge(transposed, KD * n + k + 1)
                act.activation(dst[:, k, :], ps[:, TB + k, :], ACT.Identity).then_inc(done, 1)

        def act_silu(act, f, n, ht):
            g, r = n * NHT + ht, ht % 2
            act.wait_ge(gate_ready, g + 1)
            if later(g - 1):
                act.wait_ge(hid_ready, g - 1)
            act.activation(f.silu[:, r, :], ps[:, GATE[r], :], ACT.Silu).then_inc(silu_ready, 1)

        def act_hidden_high(act, f, n, ht):
            g, r = n * NHT + ht, ht % 2
            act.wait_ge(hid_ready, g + 1)
            if ht == 0 and later(TPC * n):
                act.wait_ge(y_ready, TPC * n)
            act.activation(f.hh[:, ht, :], f.hid[:, r, :], ACT.Identity).then_inc(hh_ready, 1)

        def act_up(act, f, n, hts):
            for ht in hts:
                act_silu(act, f, n, ht)
                if ht:
                    act_hidden_high(act, f, n, ht - 1)
            if hts[-1] == NHT - 1:
                act_hidden_high(act, f, n, NHT - 1)

        def dve_x_low(dve, dst, high, n, high_done, done):
            for k in range(KD):
                dve.wait_ge(high_done, KD * n + k + 1)
                dve.tensor_tensor(dst[:, k, :], ps[:, TB + k, :], high[:, k, :].bitcast(F32), ALU.subtract)\
                   .then_inc(done, 1)

        def dve_hidden(dve, f, n, hts):
            for ht in hts:
                g, r = n * NHT + ht, ht % 2
                dve.wait_ge(silu_ready, g + 1)
                dve.wait_ge(lin_ready, g + 1)
                if later(g - 1):
                    dve.wait_ge(hl_ready, g - 1)
                dve.tensor_tensor(f.hid[:, r, :], ps[:, LIN[r], :], f.silu[:, r, :], ALU.mult).then_inc(hid_ready, 1)

        def dve_residual(dve, f, n, stored):
            for b in range(2):
                dve.wait_ge(y_ready, TPC * n + 2 * b + 2)
                if b == 0:
                    dve.wait_ge(xres_ready, n + 1)
                    if later(stored):
                        dve.wait_ge(xo_stored, stored)
                dve.tensor_tensor(f.xo[:, 2 * b:2 * b + 2, :], ps[:, YB + b, :].rearrange("p (j d) -> p j d", d=D),
                                  f.xres[:, 2 * b:2 * b + 2, :], ALU.add).then_inc(xo_ready, 1)

        def dve_keep_residual(dve, f, n):
            if later(2 * n):
                dve.wait_ge(xo_ready, 2 * n)
            dve.tensor_copy(f.xres[:], f.xin[:]).then_inc(xres_ready, 1)

        def pool_hidden_low(pool, f, n, hts):
            for ht in hts:
                g, r = n * NHT + ht, ht % 2
                pool.wait_ge(hh_ready, g + 1)
                pool.tensor_tensor(f.hl[:, ht, :], f.hid[:, r, :], f.hh[:, ht, :].bitcast(F32), ALU.subtract)\
                    .then_inc(hl_ready, 1)

        def rows(dram, c):
            return dram[bass.ts(c, CH), :].rearrange("(j p) d -> p j d", p=P)

        mid_stats, mid_var, mid_rstd, x1n_ready = sem("mid_stats"), sem("mid_var"), sem("mid_rstd"), sem("x1n_ready")
        mid_seed, mid_newton = sem("mid_seed"), sem("mid_newton")
        x1T_ready, x1h_ready, x1l_ready = sem("x1T_ready"), sem("x1h_ready"), sem("x1l_ready")
        proj_ready, qb_ready, v_ready, v_kept, v_stored = (
            sem("proj_ready"), sem("qb_ready"), sem("v_ready"), sem("v_kept"), sem("v_stored"))
        table_loaded, swap_ready, sin_ready, cos_ready, rope_ready = (
            sem("table_loaded"), sem("swap_ready"), sem("sin_ready"), sem("cos_ready"), sem("rope_ready"))
        rope_h_ready, rope_l_ready = sem("rope_h_ready"), sem("rope_l_ready")
        rope_h_stored = [sem(f"rope_h_stored{j}") for j in range(4)]
        rope_l_stored = [sem(f"rope_l_stored{j}") for j in range(4)]
        ones_ready = sem("ones_ready")
        NPJ = 2 * KD
        PIECE_BANK = (GATE[0], LIN[0], GATE[1], LIN[1])
        with ExitStack() as scope:
            f = ffn_buffers(scope, 1)
            mid = Buffers()
            mid.stats = sb("mid_stats_s", [P, TPC, 6], F32, scope)
            mid.mv = sb("mid_mv", [P, TPC, 2], F32, scope)
            mid.rstd = sb("mid_rstd_s", [P, TPC], F32, scope)
            mid.veps, mid.newt = sb("mid_veps", [P, TPC], F32, scope), sb("mid_newt", [P, TPC], F32, scope)
            mid.bits = sb("mid_bits", [P, TPC], I32, scope)
            x1n = sb("x1n", [P, TPC, D], F32, scope)
            x1h, x1l = sb("x1h", [P, KD, CH], F32R, scope), sb("x1l", [P, KD, CH], F32R, scope)
            cos_s, sin_s = sb("cos_s", [P, CH], F32, scope), sb("sin_s", [P, CH], F32, scope)
            qb = sb("qb", [P, 2, CH], F32, scope)
            swap = sb("swap", [P, 2, CH], F32, scope)
            qcos = sb("qcos", [P, 2, CH], F32, scope)
            rope = sb("rope", [P, 2, CH], F32, scope)
            rope_h, rope_l = sb("rope_h", [P, NPJ, CH], F32R, scope), sb("rope_l", [P, NPJ, CH], F32R, scope)
            vaug = sb("vaug", [P, TPC, NH, 32], F32, scope)

            with nc.Block() as block:
                @block.sync
                def _(sp):
                    def load_x(c):
                        if later(c):
                            sp.wait_ge(xres_ready, c)
                            sp.wait_ge(xn_ready, c)
                        sp.dma_start(f.xin[:], rows(x, c)).then_inc(xin_loaded, 16)

                    def load_tables(c):
                        if later(NPJ * c):
                            sp.wait_ge(rope_ready, NPJ * c)
                        sp.dma_start(cos_s[:], cos_t[:, bass.ts(c % 2, CH)]).then_inc(table_loaded, 16)
                        sp.dma_start(sin_s[:], sin_t[:, bass.ts(c % 2, CH)]).then_inc(table_loaded, 16)

                    def store_projections(c):
                        for j in range(NPJ):
                            m = NPJ * c + j
                            which, e = j // KD, j % KD
                            sp.wait_ge(rope_h_ready, m + 1)
                            sp.dma_start(qk_d[0, which, c, e * P:(e + 1) * P, :], rope_h[:, j, :].bitcast(F32))\
                              .then_inc(rope_h_stored[j], 16)
                            sp.wait_ge(rope_l_ready, m + 1)
                            sp.dma_start(qk_d[1, which, c, e * P:(e + 1) * P, :], rope_l[:, j, :].bitcast(F32))\
                              .then_inc(rope_l_stored[j], 16)
                        sp.wait_ge(v_kept, TPC * c + TPC)
                        sp.dma_start(rows(v_d, c), vaug[:].rearrange("p j h d -> p j (h d)")).then_inc(v_stored, 16)

                    def store_x1(c):
                        sp.wait_ge(xo_ready, 2 * c + 2)
                        sp.dma_start(rows(x1_d, c), f.xo[:]).then_inc(xo_stored, 16)

                    load_x(0)
                    load_x(1)
                    store_x1(0)

                    def steady(c):
                        load_x(c + 1)
                        load_tables(c - 1)
                        store_projections(c - 1)
                        store_x1(c)

                    steady(1)
                    with sp.Fori(2, NC - 1) as c:
                        steady(c)
                    load_tables(NC - 2)
                    store_projections(NC - 2)
                    store_x1(NC - 1)
                    load_tables(NC - 1)
                    store_projections(NC - 1)
                    for j in range(NPJ):
                        sp.wait_ge(rope_h_stored[j], 16 * NC)
                        sp.wait_ge(rope_l_stored[j], 16 * NC)
                    sp.wait_ge(v_stored, 16 * NC)
                    sp.wait_ge(xo_stored, 16 * NC)

                @block.tensor
                def _(pe):
                    def transpose_x(c):
                        pe.wait_ge(xn_ready, c + 1)
                        if later(TPC * (c - 1)):
                            pe.wait_ge(v_kept, TPC * (c - 1))
                        pe_transpose(pe, f.xn, xT_ready)

                    def transpose_x1(c):
                        pe.wait_ge(x1n_ready, c + 1)
                        pe_transpose(pe, x1n, x1T_ready)

                    def project(c, silu_before, hid_before):
                        pe.wait_ge(x1h_ready, KD * c + KD)
                        pe.wait_ge(x1l_ready, KD * c + KD)
                        for j in range(NPJ):
                            which, e = j // KD, j % KD
                            bank, cols = PIECE_BANK[j], slice(e * P, (e + 1) * P)
                            if j % 2 == 0:
                                pe.wait_ge(silu_ready, silu_before - 1 + j // 2)
                            else:
                                pe.wait_ge(hid_ready, hid_before - 1 + j // 2)
                            for k in range(KD):
                                pe.matmul(ps[:, bank, :], wp_h[:, which, k, cols], x1h[:, k, :], start=(k == 0), stop=False)
                                pe.matmul(ps[:, bank, :], wp_h[:, which, k, cols], x1l[:, k, :], start=False, stop=False)
                                ins = pe.matmul(ps[:, bank, :], wp_l[:, which, k, cols], x1h[:, k, :],
                                                start=False, stop=(k == KD - 1))
                            ins.then_inc(proj_ready, 1)
                        for j in range(TPC):
                            dst, cols = ps[:, TB + j // 2, (j % 2) * D:(j % 2 + 1) * D], slice(j * P, (j + 1) * P)
                            for k in range(KD):
                                pe.matmul(dst, x1h[:, k, cols], wp_h[:, 2, k, :], start=(k == 0), stop=False)
                                pe.matmul(dst, x1h[:, k, cols], wp_l[:, 2, k, :], start=False, stop=False)
                                ins = pe.matmul(dst, x1l[:, k, cols], wp_h[:, 2, k, :], start=False, stop=(k == KD - 1))
                            ins.then_inc(v_ready, 1)

                    transpose_x(0)
                    pe_up(pe, f, 0, range(NHT))
                    pe_down(pe, f, 0, (0, 1))
                    transpose_x(1)
                    pe_down(pe, f, 0, (2, 3))

                    def steady(c):
                        pe_up(pe, f, c, range(6), banks_free=(qb_ready, NPJ * (c - 1)))
                        transpose_x1(c - 1)
                        pe_up(pe, f, c, (6, 7))
                        project(c - 1, NHT * c + NHT, NHT * c + NHT)

                    def down(c):
                        pe_down(pe, f, c, (0, 1))
                        transpose_x(c + 1)
                        pe_down(pe, f, c, (2, 3))

                    steady(1)
                    down(1)
                    with pe.Fori(2, NC - 1) as c:
                        steady(c)
                        down(c)
                    steady(NC - 1)
                    pe_down(pe, f, NC - 1, range(TPC))
                    pe.wait_ge(v_kept, TPC * (NC - 1))
                    transpose_x1(NC - 1)
                    pe.wait_ge(qb_ready, NPJ * (NC - 1))
                    project(NC - 1, NHT * NC, NHT * NC)

                @block.scalar
                def _(act):
                    def biased(c, j):
                        m, r = NPJ * c + j, j % 2
                        act.wait_ge(proj_ready, m + 1)
                        if later(m - 1):
                            act.wait_ge(swap_ready, m - 1)
                            act.wait_ge(cos_ready, m - 1)
                        act.activation(qb[:, r, :], ps[:, PIECE_BANK[j], :], ACT.Identity,
                                       bias=bqk_s[:, j // KD, j % KD:j % KD + 1]).then_inc(qb_ready, 1)

                    def rope_high(c, j):
                        m, r = NPJ * c + j, j % 2
                        act.wait_ge(rope_ready, m + 1)
                        if later(16 * c):
                            act.wait_ge(rope_h_stored[j], 16 * c)
                        act.activation(rope_h[:, j, :], rope[:, r, :], ACT.Identity).then_inc(rope_h_ready, 1)

                    def projections(c):
                        biased(c, 0)
                        for j in range(1, NPJ):
                            biased(c, j)
                            rope_high(c, j - 1)
                        rope_high(c, NPJ - 1)

                    act_x_high(act, f.xh, 0, xT_ready, xh_ready)
                    act_up(act, f, 0, range(NHT))
                    act_x_high(act, f.xh, 1, xT_ready, xh_ready)

                    def steady(c):
                        act_up(act, f, c, range(6))
                        act_x_high(act, x1h, c - 1, x1T_ready, x1h_ready)
                        act_up(act, f, c, (6, 7))
                        projections(c - 1)

                    steady(1)
                    act_x_high(act, f.xh, 2, xT_ready, xh_ready)
                    with act.Fori(2, NC - 1) as c:
                        steady(c)
                        act_x_high(act, f.xh, c + 1, xT_ready, xh_ready)
                    steady(NC - 1)
                    act_x_high(act, x1h, NC - 1, x1T_ready, x1h_ready)
                    projections(NC - 1)

                @block.vector
                def _(dve):
                    def norm_in(c):
                        dve.wait_ge(xin_loaded, 16 * c + 16)
                        ln_stats(dve, f.xin, f, c, stats_ready, var_ready, seed_ready)

                    def scale_in(c):
                        if later(KD * c):
                            dve.wait_ge(xT_ready, KD * c)
                        ln_scale(dve, f.xn, f.xin, f, c, rstd_ready, xn_ready)

                    def norm_mid(c):
                        dve.wait_ge(xo_ready, 2 * c + 2)
                        ln_stats(dve, f.xo, mid, c, mid_stats, mid_var, mid_seed)

                    def scale_mid(c):
                        if later(KD * c):
                            dve.wait_ge(x1T_ready, KD * c)
                        ln_scale(dve, x1n, f.xo, mid, c, mid_rstd, x1n_ready)

                    def swap_rows(c, j):
                        m, r = NPJ * c + j, j % 2
                        dve.wait_ge(qb_ready, m + 1)
                        if later(m - 1):
                            dve.wait_ge(rope_ready, m - 1)
                        dve.sem_inc(dve_passed)
                        dve.stream_shuffle(swap[:, r, :], qb[:, r, :], [i ^ 1 for i in range(32)]).then_inc(swap_ready, 1)

                    def rotate(c, j):
                        m, r = NPJ * c + j, j % 2
                        dve.wait_ge(swap_ready, m + 1)
                        if j == 0:
                            dve.wait_ge(table_loaded, 32 * c + 32)
                        dve.tensor_tensor(swap[:, r, :], swap[:, r, :], sin_s[:], ALU.mult).then_inc(sin_ready, 1)
                        dve.wait_ge(sin_ready, m + 1)
                        dve.wait_ge(cos_ready, m + 1)
                        if later(m - 1):
                            dve.wait_ge(rope_l_ready, m - 1)
                        dve.tensor_tensor(rope[:, r, :], swap[:, r, :], qcos[:, r, :], ALU.add).then_inc(rope_ready, 1)

                    def projections(c):
                        swap_rows(c, 0)
                        for j in range(1, NPJ):
                            swap_rows(c, j)
                            rotate(c, j - 1)
                        rotate(c, NPJ - 1)
                        for j in range(TPC):
                            dve.wait_ge(v_ready, TPC * c + (j // 2) * 2 + 2)
                            if j == 0 and later(16 * c):
                                dve.wait_ge(v_stored, 16 * c)
                            dve.tensor_tensor(vaug[:, j, :, 0:DH],
                                              ps[:, TB + j // 2, (j % 2) * D:(j % 2 + 1) * D].rearrange("p (h d) -> p h d", d=DH),
                                              bvo_s[:, 0, :].rearrange("p (h d) -> p h d", d=DH), ALU.add).then_inc(v_kept, 1)

                    norm_in(0)
                    scale_in(0)
                    dve_keep_residual(dve, f, 0)
                    dve.memset(vaug[:], 1.0).then_inc(ones_ready, 1)
                    dve.wait_ge(ones_ready, 1)
                    dve_x_low(dve, f.xl, f.xh, 0, xh_ready, xl_ready)
                    dve_hidden(dve, f, 0, range(4))
                    norm_in(1)
                    dve_hidden(dve, f, 0, (4,))
                    scale_in(1)
                    dve_hidden(dve, f, 0, range(5, NHT))
                    dve_x_low(dve, f.xl, f.xh, 1, xh_ready, xl_ready)
                    dve_residual(dve, f, 0, 0)
                    dve_keep_residual(dve, f, 1)
                    norm_mid(0)

                    def steady(c, last):
                        dve_hidden(dve, f, c, range(2))
                        scale_mid(c - 1)
                        dve_hidden(dve, f, c, (2,))
                        if not last:
                            norm_in(c + 1)
                        dve_hidden(dve, f, c, (3,))
                        if not last:
                            scale_in(c + 1)
                        dve_hidden(dve, f, c, (4, 5))
                        dve_x_low(dve, x1l, x1h, c - 1, x1h_ready, x1l_ready)
                        dve_hidden(dve, f, c, (6, 7))
                        projections(c - 1)
                        if not last:
                            dve_x_low(dve, f.xl, f.xh, c + 1, xh_ready, xl_ready)
                        dve_residual(dve, f, c, 16 * c)
                        if not last:
                            dve_keep_residual(dve, f, c + 1)
                        norm_mid(c)

                    steady(1, False)
                    with dve.Fori(2, NC - 1) as c:
                        steady(c, False)
                    steady(NC - 1, True)
                    scale_mid(NC - 1)
                    dve_x_low(dve, x1l, x1h, NC - 1, x1h_ready, x1l_ready)
                    projections(NC - 1)

                @block.gpsimd
                def _(pool):
                    def times_cos(c, j):
                        m, r = NPJ * c + j, j % 2
                        if j == 0:
                            pool.wait_ge(table_loaded, 32 * c + 32)
                        pool.wait_ge(qb_ready, m + 1)
                        if later(m - 1):
                            pool.wait_ge(rope_ready, m - 1)
                        pool.tensor_tensor(qcos[:, r, :], qb[:, r, :], cos_s[:], ALU.mult).then_inc(cos_ready, 1)

                    def rope_low(c, j):
                        m, r = NPJ * c + j, j % 2
                        pool.wait_ge(rope_h_ready, m + 1)
                        if later(16 * c):
                            pool.wait_ge(rope_l_stored[j], 16 * c)
                        pool.tensor_tensor(rope_l[:, j, :], rope[:, r, :], rope_h[:, j, :].bitcast(F32), ALU.subtract)\
                            .then_inc(rope_l_ready, 1)

                    def projections(c):
                        times_cos(c, 0)
                        for j in range(1, NPJ):
                            times_cos(c, j)
                            rope_low(c, j - 1)
                        rope_low(c, NPJ - 1)

                    ln_rstd(pool, f, 0, seed_ready, newton_step, rstd_ready)
                    pool_hidden_low(pool, f, 0, range(4))
                    ln_rstd(pool, f, 1, seed_ready, newton_step, rstd_ready)
                    pool_hidden_low(pool, f, 0, range(4, NHT))
                    ln_rstd(pool, mid, 0, mid_seed, mid_newton, mid_rstd)

                    def steady(c, last):
                        pool_hidden_low(pool, f, c, range(3))
                        if not last:
                            ln_rstd(pool, f, c + 1, seed_ready, newton_step, rstd_ready)
                        pool_hidden_low(pool, f, c, range(3, NHT))
                        projections(c - 1)
                        ln_rstd(pool, mid, c, mid_seed, mid_newton, mid_rstd)

                    steady(1, False)
                    with pool.Fori(2, NC - 1) as c:
                        steady(c, False)
                    steady(NC - 1, True)
                    projections(NC - 1)

        q_loaded = [sem(f"q_loaded{a}") for a in range(3)]
        k_loaded = [sem(f"k_loaded{a}") for a in range(3)]
        vq_loaded = [sem(f"vq_loaded{a}") for a in range(3)]
        causal_loaded = sem("causal_loaded")
        constants_ready = {0: sem("constants_ready_vector"), 2: sem("constants_ready_gpsimd")}
        score_ready, max_ready, row_max_ready = sem("score_ready"), sem("max_ready"), sem("row_max_ready")
        negmax_loaded = [sem(f"negmax_loaded{r}") for r in range(2)]
        keyed_ready, prob_ready, masked_ready = sem("keyed_ready"), sem("prob_ready"), sem("masked_ready")
        pv_ready, att_ready, att_stored = sem("pv_ready"), sem("att_ready"), sem("att_stored")
        sums_loaded, rec_ready, rec_stored = sem("sums_loaded"), sem("rec_ready"), sem("rec_stored")
        KEYED, SCORE, ATT = 0, 3, 6
        STEPS = 4 * NB
        PIECES = []
        for i in range(NB):
            w = P * (i + 1)
            if w <= CH:
                PIECES.append((i, 0, w, max(w, 256), True))
            else:
                first = 384 if w == 640 else CH
                PIECES.append((i, 0, first, first, False))
                PIECES.append((i, first, w - first, max(w - first, 256), True))
        NP = len(PIECES)
        PER_HEAD = NP + 1
        ORDER = []
        for h in range(4):
            for k in range(NP):
                ORDER.append(("piece", h, k))
                if h and k == 2:
                    ORDER.append(("turn", h - 1, 0))
        ORDER.append(("turn", 3, 0))
        NO = len(ORDER)
        SHARE = (6, 8, 7, 7, 7, 7, 7, 3)
        STEP_PIECES = [(2 if S - (k // 4) * P > CH else 1) for k in range(STEPS)]
        PIECE_AT = [sum(STEP_PIECES[:k]) for k in range(STEPS + 1)]
        NK = PIECE_AT[STEPS]
        TURN_AT = [ORDER.index(("turn", h, 0)) for h in range(4)]
        with ExitStack() as scope:
            qst = [[sb(f"qst{a}{g}", [P, S], F32R, scope) for g in range(2)] for a in range(3)]
            kst = [[sb(f"kst{a}{h}", [P, S], F32R, scope) for h in range(4)] for a in range(3)]
            vq = [sb(f"vq{a}", [P, NB, 4, 32], F32, scope) for a in range(3)]
            prob = sb("prob", [P, 8, S], F32, scope)
            causal_s = sb("causal_s", [P, CH], F32, scope)
            junk = sb("junk", [P, 3, CH], F32, scope)
            part_max = sb("part_max", [P, 2, 16], F32, scope)
            negmax = sb("negmax", [NB, 2, P], F32R, scope)
            att = sb("att", [P, 2, CH], F32, scope)
            sums, rec = sb("sums", [P, 32], F32, scope), sb("rec", [P, 32], F32, scope)

            CONSTANTS = 5
            def stack_constants(eng, heads):
                ready = constants_ready[heads[0]]
                for a in range(3):
                    even, odd = kst[a][heads[0]], kst[a][heads[1]]
                    for m, (rows_, value) in enumerate(((even[:], 0.0), (even[96:97, :], 1.0), (odd[:], 0.0),
                                                        (odd[96:98, :], 1.0), (odd[96:97, :], 0.0))):
                        if CONSTANTS * a + m:
                            eng.wait_ge(ready, CONSTANTS * a + m)
                        eng.memset(rows_.bitcast(F32), value).then_inc(ready, 1)

            with nc.Block() as block:
                @block.sync
                def _(sp):
                    def load_quad(q, a):
                        b, u = q // 4, q % 4
                        if later(q - 2):
                            sp.wait_ge(pv_ready, NB * (q - 2))
                        for part, row in ((0, 0), (1, 32), (0, 64)):
                            for g in range(2):
                                sp.dma_start(qst[a][g][row:row + 32, :].bitcast(F32).rearrange("r (u t) -> r u t", u=2),
                                             qk_d[part, 0, bass.ds(2 * b, 2), bass.ds(64 * u + 32 * g, 32), :]
                                             .rearrange("u r t -> r u t")).then_inc(q_loaded[a], 16)
                        for part, row in ((0, 0), (0, 32), (1, 64)):
                            for h in range(4):
                                r = row + DH * (h % 2)
                                sp.dma_start(kst[a][h][r:r + DH, :].bitcast(F32).rearrange("r (u t) -> r u t", u=2),
                                             qk_d[part, 1, bass.ds(2 * b, 2), bass.ds(64 * u + DH * h, DH), :]
                                             .rearrange("u r t -> r u t")).then_inc(k_loaded[a], 16)
                        sp.dma_start(vq[a][:].rearrange("p n h d -> p n (h d)"),
                                     v_d[bass.ts(b, S), bass.ts(u, P)].rearrange("(n p) f -> p n f", p=P))\
                          .then_inc(vq_loaded[a], 16)

                    def load_negmax(q, a):
                        for h in range(4):
                            sp.wait_ge(max_ready, NO * q + TURN_AT[h] + 1)
                            sp.dma_start(qst[a][h // 2][96 + h % 2:97 + h % 2, :].bitcast(F32),
                                         negmax[:, h % 2, :].bitcast(F32)).then_inc(negmax_loaded[h % 2], 16)

                    def store_att(q, half):
                        b, u = q // 4, q % 4
                        sp.wait_ge(att_ready, 2 * q + half + 1)
                        for h in range(4):
                            sp.dma_start(att_d[2 * b + half, bass.ds(64 * u + DH * h, DH), :],
                                         att[32 * h:32 * h + DH, half, :]).then_inc(att_stored, 16)
                            sp.dma_start(sums[32 * h + 16 * half:32 * h + 16 * half + 16, :],
                                         att[32 * h + DH:32 * h + DH + 1, half, :]).then_inc(sums_loaded, 16)

                    def store_rec(q):
                        sp.wait_ge(rec_ready, q + 1)
                        sp.dma_start(rec_d[q, :, :].rearrange("h (p n) -> (h p) n", n=32), rec[:])\
                          .then_inc(rec_stored, 16)

                    sp.dma_start(causal_s[:], causal).then_inc(causal_loaded, 16)
                    for a in range(2):
                        for ready in constants_ready.values():
                            sp.wait_ge(ready, CONSTANTS * (a + 1))
                        load_quad(a, a)
                    for ready in constants_ready.values():
                        sp.wait_ge(ready, CONSTANTS * 3)
                    load_negmax(0, 0)

                    def slot(q, a, last=0):
                        if last < 1:
                            load_quad(q + 2, (a + 2) % 3)
                        if last < 2:
                            load_negmax(q + 1, (a + 1) % 3)
                        if later(q):
                            store_rec(q - 1)
                        store_att(q, 0)
                        store_att(q, 1)

                    for q in range(3):
                        slot(q, q)
                    with sp.Fori(1, QUADS // 3 - 1) as j:
                        for a in range(3):
                            slot(3 * j + a, a)
                    slot(QUADS - 4, 0)
                    slot(QUADS - 3, 1)
                    slot(QUADS - 2, 2, last=1)
                    slot(QUADS - 1, 0, last=2)
                    store_rec(QUADS - 1)
                    sp.wait_ge(att_stored, 16 * 8 * QUADS)
                    sp.wait_ge(rec_stored, 16 * QUADS)

                @block.tensor
                def _(pe):
                    def first_pass(q, a, j, n):
                        kind, h, k = ORDER[n]
                        s, bank = NO * q + n, SCORE + (NO * a + n) % 3
                        if n == 0:
                            pe.wait_ge(q_loaded[a], 16 * 6 * (j + 1))
                            pe.wait_ge(k_loaded[a], 16 * 12 * (j + 1))
                        if later(s - 2):
                            pe.wait_ge(max_ready, s - 2)
                        if kind == "piece":
                            i, t0, _, cols, _ = PIECES[k]
                            pe.matmul(ps[:, bank, 0:cols], qst[a][h // 2][0:96, i * P:(i + 1) * P],
                                      kst[a][h][0:96, t0:t0 + cols], start=True, stop=True).then_inc(score_ready, 1)
                        else:
                            pe.wait_ge(row_max_ready, 4 * q + h + 1)
                            pe.transpose(ps[0:NB, bank, 0:P], part_max[:, h % 2, 0:NB], ident[:]).then_inc(score_ready, 1)

                    def keyed(q, a, i, h):
                        if i == 0:
                            pe.wait_ge(negmax_loaded[h % 2], 16 * (2 * q + h // 2 + 1))
                        w = S - i * P
                        rows_used = 97 + h % 2
                        lhs = kst[a][h][0:rows_used, i * P:(i + 1) * P]
                        n = STEP_PIECES[4 * i + h]
                        for b in range(n):
                            at = PIECE_AT[4 * i + h] + b
                            if later(NK * q + at - 2):
                                pe.wait_ge(prob_ready, NK * q + at - 2)
                            cols = w // n
                            s0 = i * P + b * cols
                            if cols < 256:
                                s0, cols = S - 256, 256
                            pe.matmul(ps[:, KEYED + at % 3, 0:cols], lhs, qst[a][h // 2][0:rows_used, s0:s0 + cols],
                                      start=True, stop=True).then_inc(keyed_ready, 1)

                    def values(q, a, j, i, halves):
                        if i == 0 and 0 in halves:
                            pe.wait_ge(vq_loaded[a], 16 * (j + 1))
                        pe.wait_ge(prob_ready, NK * q + PIECE_AT[4 * i + 4])
                        pe.wait_ge(masked_ready, STEPS * q + 4 * i + 4)
                        for half in halves:
                            if half * CH + CH <= i * P:
                                continue
                            if i == 0 and later(2 * q - 1 + half):
                                pe.wait_ge(att_ready, 2 * q - 1 + half)
                            first = max(i * P, half * CH)
                            for h in range(4):
                                ins = pe.matmul(ps[32 * h:32 * h + 32, ATT + half, first - half * CH:CH],
                                                vq[a][:, i, h, :],
                                                prob[:, 4 * (i % 2) + h, first - i * P:half * CH + CH - i * P],
                                                start=(i == 0), stop=(i == 4 * half + 3), tile_position=(0, 32 * h))
                        if 1 in halves:
                            ins.then_inc(pv_ready, 1)

                    for n in range(NO):
                        first_pass(0, 0, 0, n)

                    def slot(q, a, j, more=True):
                        n = 0
                        for k in range(STEPS):
                            i, h = k // 4, k % 4
                            keyed(q, a, i, h)
                            if more:
                                for _ in range(SHARE[i] * (h + 1) // 4 - SHARE[i] * h // 4):
                                    first_pass(q + 1, (a + 1) % 3, j + (a + 1) // 3, n)
                                    n += 1
                            if i and h == 1:
                                values(q, a, j, i - 1, (0,))
                            if i and h == 2:
                                values(q, a, j, i - 1, (1,))
                        values(q, a, j, NB - 1, (0, 1))

                    for q in range(3):
                        slot(q, q, 0)
                    with pe.Fori(1, QUADS // 3) as j:
                        for a in range(3):
                            slot(3 * j + a, a, j)
                    slot(QUADS - 1, 0, QUADS // 3, more=False)

                @block.scalar
                def _(act):
                    def exponential(q, i, h):
                        if h == 0 and later(NB * q + i - 1):
                            act.wait_ge(pv_ready, NB * q + i - 1)
                        w = S - i * P
                        n = STEP_PIECES[4 * i + h]
                        skip = 256 - w if w < 256 else 0
                        cols = w // n
                        for b in range(n):
                            at = PIECE_AT[4 * i + h] + b
                            act.wait_ge(keyed_ready, NK * q + at + 1)
                            act.activation(prob[:, 4 * (i % 2) + h, b * cols:(b + 1) * cols],
                                           ps[:, KEYED + at % 3, skip:skip + cols], ACT.Exp, scale=SCALE)\
                               .then_inc(prob_ready, 1)

                    def evacuate(q, half):
                        act.wait_ge(pv_ready, NB * q + 4 * half + 4)
                        if later(q):
                            act.wait_ge(att_stored, 16 * 8 * q)
                            act.wait_ge(sums_loaded, 16 * 8 * q)
                        act.activation(att[:, half, :], ps[:, ATT + half, :], ACT.Identity).then_inc(att_ready, 1)

                    def slot(q):
                        for k in range(STEPS):
                            i, h = k // 4, k % 4
                            if i == 5 and h == 0:
                                evacuate(q, 0)
                            exponential(q, i, h)
                        evacuate(q, 1)

                    slot(0)
                    slot(1)
                    with act.Fori(1, QUADS // 2) as j:
                        slot(2 * j)
                        slot(2 * j + 1)

                @block.vector
                def _(dve):
                    stack_constants(dve, (0, 1))
                    dve.wait_ge(causal_loaded, 16)

                    def first_pass(q, a, n):
                        kind, h, k = ORDER[n]
                        ring = (NO * a + n) % 3
                        s, bank, m = NO * q + n, SCORE + ring, part_max[:, h % 2, :]
                        dve.wait_ge(score_ready, s + 1)
                        if kind == "turn":
                            if later(2 * q + h // 2):
                                dve.wait_ge(negmax_loaded[h % 2], 16 * (2 * q + h // 2))
                            dve.tensor_scalar(negmax[:, h % 2, :], ps[0:NB, bank, 0:P], -1.0, None, ALU.mult)\
                               .then_inc(max_ready, 1)
                            return
                        i, _, keys, _, diagonal = PIECES[k]
                        to = m[:, i:i + 1] if i < 4 or not diagonal else m[:, 4 + i:5 + i]
                        if diagonal:
                            dve.sem_inc(dve_passed)
                            dve.tensor_tensor_reduce(junk[:, ring, 0:keys], ps[:, bank, 0:keys], causal_s[:, CH - keys:CH],
                                                     1.0, -3e38, ALU.add, ALU.max, to).then_inc(max_ready, 1)
                        else:
                            dve.tensor_reduce(to, ps[:, bank, 0:keys], AX.X, ALU.max).then_inc(max_ready, 1)
                        if k == NP - 1:
                            dve.wait_ge(max_ready, s + 1)
                            dve.tensor_tensor(m[:, 4:8], m[:, 4:8], m[:, 8:12], ALU.max).then_inc(row_max_ready, 1)

                    def reciprocal(q):
                        dve.wait_ge(sums_loaded, 16 * 8 * (q + 1))
                        if later(q):
                            dve.wait_ge(rec_stored, 16 * q)
                        dve.reciprocal(rec[:], sums[:]).then_inc(rec_ready, 1)

                    for n in range(NO):
                        first_pass(0, 0, n)

                    def slot(q, a):
                        for n in range(NO // 2):
                            first_pass(q + 1, (a + 1) % 3, n)
                        if later(q):
                            reciprocal(q - 1)
                        for n in range(NO // 2, NO):
                            first_pass(q + 1, (a + 1) % 3, n)

                    for q in range(3):
                        slot(q, q)
                    with dve.Fori(1, QUADS // 3) as j:
                        for a in range(3):
                            slot(3 * j + a, a)
                    reciprocal(QUADS - 2)
                    reciprocal(QUADS - 1)

                @block.gpsimd
                def _(pool):
                    stack_constants(pool, (2, 3))
                    pool.wait_ge(constants_ready[2], CONSTANTS * 3)
                    with pool.Fori(0, QUADS) as q:
                        for k in range(STEPS):
                            i, h = k // 4, k % 4
                            pool.wait_ge(prob_ready, NK * q + PIECE_AT[k] + 1)
                            pool.sem_inc(pool_passed)
                            block_ = prob[:, 4 * (i % 2) + h, 0:P]
                            pool.affine_select(out=block_, in_=block_, compare_op=ALU.is_ge, fill=0.0, base=0,
                                               pattern=[[1, P]], channel_multiplier=-1).then_inc(masked_ready, 1)

        rec_loaded, att_loaded, bias_ready, norm_ready = sem("rec_loaded"), sem("att_loaded"), sem("bias_ready"), sem("norm_ready")
        ah_ready, al_ready, wo_ready, x2_ready = sem("ah_ready"), sem("al_ready"), sem("wo_ready"), sem("x2_ready")
        with ExitStack() as scope:
            f = ffn_buffers(scope, 3)
            attn = sb("attn", [P, KD, CH], F32, scope)
            inv = sb("inv", [P, KD, CH], F32, scope)
            ah, al = sb("ah", [P, KD, CH], F32R, scope), sb("al", [P, KD, CH], F32R, scope)

            with nc.Block() as block:
                @block.sync
                def _(sp):
                    def load_x(c):
                        if later(c):
                            sp.wait_ge(xres_ready, NC + c)
                            sp.wait_ge(xn_ready, NC + c)
                        sp.dma_start(f.xin[:], rows(x1_d, c)).then_inc(xin_loaded, 16)

                    def load_attention(c):
                        b, half = c // 2, c % 2
                        if later(c):
                            sp.wait_ge(al_ready, KD * c)
                        for k in range(KD):
                            sp.dma_start(attn[:, k, :], att_d[c, k * P:(k + 1) * P, :]).then_inc(att_loaded, 16)
                            for h in range(8):
                                sp.dma_start(inv[DH * h:DH * (h + 1), k, :],
                                             rec_d[4 * b + 2 * k + h // 4, h % 4, bass.ts(half, CH)].partition_broadcast(DH))\
                                  .then_inc(rec_loaded, 16)

                    def store(c):
                        sp.wait_ge(xo_ready, 2 * (NC + c) + 2)
                        sp.dma_start(rows(out, c), f.xo[:]).then_inc(xo_stored, 16)

                    load_attention(0)
                    load_x(0)
                    load_attention(1)
                    with sp.Fori(0, NC - 2) as c:
                        load_x(c + 1)
                        load_attention(c + 2)
                        store(c)
                    load_x(NC - 1)
                    store(NC - 2)
                    store(NC - 1)
                    sp.wait_ge(xo_stored, 16 * 2 * NC)

                @block.tensor
                def _(pe):
                    def project(c):
                        pe.wait_ge(ah_ready, KD * c + KD)
                        pe.wait_ge(al_ready, KD * c + KD)
                        for j in range(TPC):
                            dst, cols = ps[:, TB + j // 2, (j % 2) * D:(j % 2 + 1) * D], slice(j * P, (j + 1) * P)
                            for k in range(KD):
                                pe.matmul(dst, ah[:, k, cols], wp_h[:, 3, k, :], start=(k == 0), stop=False)
                                pe.matmul(dst, ah[:, k, cols], wp_l[:, 3, k, :], start=False, stop=False)
                                ins = pe.matmul(dst, al[:, k, cols], wp_h[:, 3, k, :], start=False, stop=(k == KD - 1))
                            ins.then_inc(wo_ready, 1)

                    def transpose_x(c):
                        pe.wait_ge(xn_ready, NC + c + 1)
                        pe_transpose(pe, f.xn, xT_ready)

                    project(0)
                    transpose_x(0)
                    with pe.Fori(0, NC - 1) as c:
                        pe_up(pe, f, NC + c, range(4))
                        project(c + 1)
                        pe_up(pe, f, NC + c, range(4, NHT))
                        pe_down(pe, f, NC + c, (0, 1))
                        transpose_x(c + 1)
                        pe_down(pe, f, NC + c, (2, 3))
                    pe_up(pe, f, 2 * NC - 1, range(NHT))
                    pe_down(pe, f, 2 * NC - 1, range(TPC))

                @block.scalar
                def _(act):
                    def split(c):
                        for k in range(KD):
                            act.wait_ge(norm_ready, KD * c + k + 1)
                            if k == 0 and later(TPC * c):
                                act.wait_ge(wo_ready, TPC * c)
                            act.activation(ah[:, k, :], attn[:, k, :], ACT.Identity).then_inc(ah_ready, 1)

                    split(0)
                    act_x_high(act, f.xh, NC, xT_ready, xh_ready)
                    with act.Fori(0, NC - 1) as c:
                        act_up(act, f, NC + c, (0, 1))
                        split(c + 1)
                        act_up(act, f, NC + c, range(2, NHT))
                        act_x_high(act, f.xh, NC + c + 1, xT_ready, xh_ready)
                    act_up(act, f, 2 * NC - 1, range(NHT))

                @block.vector
                def _(dve):
                    def normalise(c):
                        dve.wait_ge(att_loaded, 16 * KD * (c + 1))
                        dve.wait_ge(rec_loaded, 16 * 8 * KD * (c + 1))
                        for k in range(KD):
                            dve.tensor_tensor(attn[:, k, :], attn[:, k, :], inv[:, k, :], ALU.mult).then_inc(norm_ready, 1)

                    def attention_out(c):
                        for j in range(TPC):
                            dve.wait_ge(wo_ready, TPC * c + (j // 2) * 2 + 2)
                            dve.wait_ge(bias_ready, TPC * c + j + 1)
                            dve.tensor_tensor(f.xin[:, j, :], ps[:, TB + j // 2, (j % 2) * D:(j % 2 + 1) * D],
                                              f.xin[:, j, :], ALU.add).then_inc(x2_ready, 1)
                        dve.wait_ge(x2_ready, TPC * c + TPC)
                        ln_stats(dve, f.xin, f, NC + c, stats_ready, var_ready, seed_ready)

                    def scale_in(c):
                        dve.wait_ge(xT_ready, KD * (NC + c))
                        ln_scale(dve, f.xn, f.xin, f, NC + c, rstd_ready, xn_ready)

                    normalise(0)
                    attention_out(0)
                    scale_in(0)
                    dve_keep_residual(dve, f, NC)
                    dve_x_low(dve, f.xl, f.xh, NC, xh_ready, xl_ready)
                    with dve.Fori(0, NC - 1) as c:
                        n = NC + c
                        dve_hidden(dve, f, n, (0,))
                        normalise(c + 1)
                        dve_hidden(dve, f, n, range(1, 4))
                        attention_out(c + 1)
                        dve_hidden(dve, f, n, (4, 5))
                        scale_in(c + 1)
                        dve_hidden(dve, f, n, (6, 7))
                        dve_x_low(dve, f.xl, f.xh, n + 1, xh_ready, xl_ready)
                        dve_residual(dve, f, n, 16 * n)
                        dve_keep_residual(dve, f, n + 1)
                    dve_hidden(dve, f, 2 * NC - 1, range(NHT))
                    dve_residual(dve, f, 2 * NC - 1, 16 * (2 * NC - 1))

                @block.gpsimd
                def _(pool):
                    def split(c):
                        for k in range(KD):
                            pool.wait_ge(ah_ready, KD * c + k + 1)
                            pool.tensor_tensor(al[:, k, :], attn[:, k, :], ah[:, k, :].bitcast(F32), ALU.subtract)\
                                .then_inc(al_ready, 1)

                    def add_bias(c):
                        pool.wait_ge(xin_loaded, 16 * (NC + c + 1))
                        for j in range(TPC):
                            pool.tensor_tensor(f.xin[:, j, :], f.xin[:, j, :], bvo_s[:, 1, :], ALU.add).then_inc(bias_ready, 1)

                    split(0)
                    add_bias(0)
                    ln_rstd(pool, f, NC, seed_ready, newton_step, rstd_ready)
                    with pool.Fori(0, NC - 1) as c:
                        pool_hidden_low(pool, f, NC + c, (0,))
                        split(c + 1)
                        add_bias(c + 1)
                        pool_hidden_low(pool, f, NC + c, range(1, 4))
                        ln_rstd(pool, f, NC + c + 1, seed_ready, newton_step, rstd_ready)
                        pool_hidden_low(pool, f, NC + c, range(4, NHT))
                    pool_hidden_low(pool, f, 2 * NC - 1, range(NHT))


def rotary_tables():
    pos = np.arange(S, dtype=np.float32)
    theta = np.power(np.float32(10000.0), -np.arange(0, DH, 2, dtype=np.float32) / np.float32(DH)).astype(np.float32)
    angle = pos[None, :] * np.repeat(theta, 2)[:, None]
    sign = np.where(np.arange(DH) % 2 == 0, -1.0, 1.0).astype(np.float32)[:, None]
    return np.tile(np.cos(angle), (P // DH, 1)), np.tile(np.sin(angle) * sign, (P // DH, 1))


def hadamard_matrix(n):
    h = np.ones((1, 1), np.float32)
    while h.shape[0] < n:
        h = np.block([[h, h], [h, -h]])
    return h.astype(np.float32)


def kernel(**inputs):
    import concourse.bacc as bacc
    from concourse.bass_utils import run_bass_kernel_spmd

    a = {k: np.asarray(v) for k, v in inputs.items()}
    c = np.ascontiguousarray
    cos, sin = rotary_tables()
    causal = np.zeros((P, CH), np.float32)
    causal[:, CH - P:] = np.where(np.arange(P)[None, :] > np.arange(P)[:, None], NEG, 0.0)
    arrays = {
        "x": c(a["L0_attn_x"].reshape(TOK, D)),
        "w1t": c(a["L0_ffn_W1"].T), "w3t": c(a["L0_ffn_W3"].T), "w2t": c(a["L0_ffn_W2"].T),
        "wqkvo": np.stack([a["L0_attn_Wq"], a["L0_attn_Wk"], a["L0_attn_Wv"], a["L0_attn_Wo"]]),
        "bqk": c(np.stack([a["L0_attn_bq"], a["L0_attn_bk"]]).reshape(2, KD, P).transpose(2, 0, 1)),
        "bvo": c(np.broadcast_to(np.stack([a["L0_attn_bv"], a["L0_attn_bo"]]), (P, 2, D))),
        "cos_t": c(cos.astype(np.float32)), "sin_t": c(sin.astype(np.float32)),
        "hadamard": hadamard_matrix(P), "identity": np.eye(P, dtype=np.float32), "causal": causal,
    }
    nc = bacc.Bacc("TRN2", target_bir_lowering=False, num_devices=1)
    args = [nc.dram_tensor(k, v.shape, mybir.dt.from_np(v.dtype), kind="ExternalInput").ap() for k, v in arrays.items()]
    out = nc.dram_tensor("out", (TOK, D), F32, kind="ExternalOutput").ap()
    build_program(nc, *args, out)
    r = run_bass_kernel_spmd(nc, [arrays], core_ids=[0])
    return r.results[0]["out"].reshape(B, S, D)
```

```python
from contextlib import ExitStack

import numpy as np

import concourse.bass as bass
from concourse import mybir

F32 = mybir.dt.float32
F32R = mybir.dt.float32r
I32 = mybir.dt.int32
ALU = mybir.AluOpType
ACT = mybir.ActivationFunctionType
AX = mybir.AxisListType

P = 128
B, S, D = 4, 1024, 256
HID = 1024
NH = 16
DH = D // NH
TOK = B * S
CH = 512
NC = TOK // CH
TPC = CH // P
KD = D // P
NHT = HID // P
EPS = 1e-5
QUADS = B * NH // 4
NB = S // P
NEG = -1e38
SCALE = float(DH) ** -0.5


def later(value):
    return not isinstance(value, int) or value > 0


def build_program(nc, x, w1t, w3t, w2t, wqkvo, bqk, bvo, cos_t, sin_t, hadamard, identity, causal, out):
    with ExitStack() as ctx:
        def sb(name, shape, dt=F32, scope=ctx):
            return scope.enter_context(nc.sbuf_tensor(name, shape, dt))

        def sem(name):
            return ctx.enter_context(nc.semaphore(name))

        dve_passed, pool_passed = sem("dve_passed"), sem("pool_passed")

        qk_d = nc.dram_tensor("qk_scratch", [2, 2, NC, D, CH], F32, kind="Internal").ap()
        v_d = nc.dram_tensor("v_scratch", [TOK, NH * 32], F32, kind="Internal").ap()
        x1_d = nc.dram_tensor("x1_scratch", [TOK, D], F32, kind="Internal").ap()
        att_d = nc.dram_tensor("att_scratch", [NC, D, CH], F32, kind="Internal").ap()
        rec_d = nc.dram_tensor("rec_scratch", [QUADS, 4, S], F32, kind="Internal").ap()

        head_d = nc.dram_tensor("head_scratch", [2, 2, S], F32, kind="Internal").ap()

        w1_h, w1_l = sb("w1_h", [P, KD, HID], F32R), sb("w1_l", [P, KD, HID], F32R)
        w3_h, w3_l = sb("w3_h", [P, KD, HID], F32R), sb("w3_l", [P, KD, HID], F32R)
        w2_h, w2_l = sb("w2_h", [P, NHT, D], F32R), sb("w2_l", [P, NHT, D], F32R)
        wp_h, wp_l = sb("wp_h", [P, 4, KD, D], F32R), sb("wp_l", [P, 4, KD, D], F32R)
        ident = sb("ident", [P, P])
        bqk_s = sb("bqk_s", [P, 2, KD])
        bvo_s = sb("bvo_s", [P, 2, D])
        att = sb("att", [P, 2, CH])
        sums, rec = sb("sums", [P, 32]), sb("rec", [P, 32])
        causal_s = sb("causal_s", [P, CH])
        junk = sb("junk", [P, 3, CH])
        part_max = sb("part_max", [P, 2, 16])
        negmax = sb("negmax", [NB, 2, P], F32R)
        ps = ctx.enter_context(nc.psum_tensor("ps", [P, 8, CH], F32))
        GATE, LIN, YB, TB = (0, 1), (2, 3), 4, 6

        xin_loaded, xres_ready = sem("xin_loaded"), sem("xres_ready")
        stats_ready, var_ready, rstd_ready, xn_ready = sem("stats_ready"), sem("var_ready"), sem("rstd_ready"), sem("xn_ready")
        seed_ready, newton_step = sem("seed_ready"), sem("newton_step")
        xT_ready, xh_ready, xl_ready = sem("xT_ready"), sem("xh_ready"), sem("xl_ready")
        gate_ready, lin_ready, silu_ready, hid_ready = sem("gate_ready"), sem("lin_ready"), sem("silu_ready"), sem("hid_ready")
        hh_ready, hl_ready, y_ready, xo_ready, xo_stored = (
            sem("hh_ready"), sem("hl_ready"), sem("y_ready"), sem("xo_ready"), sem("xo_stored"))

        class Buffers:
            pass

        def ln_buffers(b, t):
            b.stats, b.mv = sb(f"stats{t}", [P, TPC, 6]), sb(f"mv{t}", [P, TPC, 2])
            b.rstd, b.veps, b.newt = sb(f"rstd{t}", [P, TPC]), sb(f"veps{t}", [P, TPC]), sb(f"newt{t}", [P, TPC])
            b.bits = sb(f"bits{t}", [P, TPC], I32)

        def input_buffers(f, scope, t):
            f.xin = sb(f"xin{t}", [P, TPC, D], F32, scope)
            f.xn = sb(f"xn{t}", [P, TPC, D], F32, scope)
            f.xh = sb(f"xh{t}", [P, KD, CH], F32R, scope)
            f.xl = sb(f"xl{t}", [P, KD, CH], F32R, scope)

        def ffn_buffers(f, scope, t):
            f.xres = sb(f"xres{t}", [P, TPC, D], F32, scope)
            f.silu = sb(f"silu{t}", [P, 2, CH], F32, scope)
            f.hid = sb(f"hid{t}", [P, 2, CH], F32, scope)
            f.hh = sb(f"hh{t}", [P, NHT, CH], F32R, scope)
            f.hl = sb(f"hl{t}", [P, NHT, CH], F32R, scope)
            f.xo = sb(f"xo{t}", [P, TPC, D], F32, scope)

        def ln_stats(dve, src, f, n, stats_done, var_done, seed_done):
            for j in range(TPC):
                dve.bn_stats(f.stats[:, j, :], src[:, j, :]).then_inc(stats_done, 1)
            for j in range(TPC):
                dve.wait_ge(stats_done, TPC * n + j + 1)
                dve.sem_inc(dve_passed)
                dve.bn_aggr(f.mv[:, j, :], f.stats[:, j, :]).then_inc(var_done, 1)
            dve.wait_ge(var_done, TPC * n + TPC)
            dve.tensor_scalar(f.veps[:], f.mv[:, :, 1], EPS, None, ALU.add).then_inc(seed_done, 1)
            dve.wait_ge(seed_done, 3 * n + 1)
            dve.tensor_scalar(f.bits[:], f.veps[:].bitcast(I32), 1, None, ALU.logical_shift_right).then_inc(seed_done, 1)
            dve.wait_ge(seed_done, 3 * n + 2)
            dve.tensor_scalar(f.rstd[:].bitcast(I32), f.bits[:], -1.0, float(0x5F3759DF), ALU.mult, ALU.add)\
               .then_inc(seed_done, 1)

        def ln_rstd(pool, f, n, seed_done, newton_done, rstd_done):
            pool.wait_ge(seed_done, 3 * n + 3)
            done = 11 * n
            for step in range(3):
                last = step == 2
                if step:
                    pool.wait_ge(newton_done, done)
                pool.tensor_tensor(f.newt[:], f.rstd[:], f.rstd[:], ALU.mult).then_inc(newton_done, 1)
                pool.wait_ge(newton_done, done + 1)
                pool.tensor_tensor(f.newt[:], f.newt[:], f.veps[:], ALU.mult).then_inc(newton_done, 1)
                pool.wait_ge(newton_done, done + 2)
                pool.sem_inc(pool_passed)
                pool.tensor_scalar(f.newt[:], f.newt[:], -0.5, 1.5, ALU.mult, ALU.add).then_inc(newton_done, 1)
                pool.wait_ge(newton_done, done + 3)
                pool.tensor_tensor(f.rstd[:], f.rstd[:], f.newt[:], ALU.mult).then_inc(rstd_done if last else newton_done, 1)
                done = done + 4

        def ln_scale(dve, dst, src, f, n, rstd_done, done):
            dve.wait_ge(rstd_done, n + 1)
            for j in range(TPC):
                ins = dve.tensor_scalar(dst[:, j, :], src[:, j, :], f.mv[:, j, 0:1], f.rstd[:, j:j + 1],
                                        ALU.subtract, ALU.mult)
            ins.then_inc(done, 1)

        def pe_transpose(pe, src, done, bank=TB):
            for k in range(KD):
                for j in range(TPC):
                    ins = pe.transpose(ps[:, bank + k, j * P:(j + 1) * P], src[:, j, k * P:(k + 1) * P], ident[:])
                ins.then_inc(done, 1)

        def pe_up(pe, f, n, hts, banks_free=None):
            for ht in hts:
                g, r = n * NHT + ht, ht % 2
                if ht == 0:
                    pe.wait_ge(xh_ready, KD * n + KD)
                    pe.wait_ge(xl_ready, KD * n + KD)
                    if banks_free is not None and later(banks_free[1]):
                        pe.wait_ge(*banks_free)
                for w_h, w_l, bank, freed, done in ((w1_h, w1_l, GATE[r], silu_ready, gate_ready),
                                                    (w3_h, w3_l, LIN[r], hid_ready, lin_ready)):
                    if later(g - 1):
                        pe.wait_ge(freed, g - 1)
                    cols = slice(ht * P, (ht + 1) * P)
                    for k in range(KD):
                        pe.matmul(ps[:, bank, :], w_h[:, k, cols], f.xh[:, k, :], start=(k == 0), stop=False)
                        pe.matmul(ps[:, bank, :], w_h[:, k, cols], f.xl[:, k, :], start=False, stop=False)
                        ins = pe.matmul(ps[:, bank, :], w_l[:, k, cols], f.xh[:, k, :], start=False, stop=(k == KD - 1))
                    ins.then_inc(done, 1)

        def pe_down(pe, f, n, tiles):
            for j in tiles:
                dst = ps[:, YB + j // 2, (j % 2) * D:(j % 2 + 1) * D]
                if j % 2 == 0 and later(2 * n - 1 + j // 2):
                    pe.wait_ge(xo_ready, 2 * n - 1 + j // 2)
                for ht in range(NHT):
                    if j == 0:
                        pe.wait_ge(hh_ready, NHT * n + ht + 1)
                        pe.wait_ge(hl_ready, NHT * n + ht + 1)
                    cols = slice(j * P, (j + 1) * P)
                    pe.matmul(dst, f.hh[:, ht, cols], w2_h[:, ht, :], start=(ht == 0), stop=False)
                    pe.matmul(dst, f.hh[:, ht, cols], w2_l[:, ht, :], start=False, stop=False)
                    ins = pe.matmul(dst, f.hl[:, ht, cols], w2_h[:, ht, :], start=False, stop=(ht == NHT - 1))
                ins.then_inc(y_ready, 1)

        def act_x_high(act, dst, n, transposed, done, bank=TB):
            for k in range(KD):
                act.wait_ge(transposed, KD * n + k + 1)
                act.activation(dst[:, k, :], ps[:, bank + k, :], ACT.Identity).then_inc(done, 1)

        def act_silu(act, f, n, ht):
            g, r = n * NHT + ht, ht % 2
            act.wait_ge(gate_ready, g + 1)
            if later(g - 1):
                act.wait_ge(hid_ready, g - 1)
            act.activation(f.silu[:, r, :], ps[:, GATE[r], :], ACT.Silu).then_inc(silu_ready, 1)

        def act_hidden_high(act, f, n, ht):
            g, r = n * NHT + ht, ht % 2
            act.wait_ge(hid_ready, g + 1)
            if ht == 0 and later(TPC * n):
                act.wait_ge(y_ready, TPC * n)
            act.activation(f.hh[:, ht, :], f.hid[:, r, :], ACT.Identity).then_inc(hh_ready, 1)

        def act_up(act, f, n, hts):
            for ht in hts:
                act_silu(act, f, n, ht)
                if ht:
                    act_hidden_high(act, f, n, ht - 1)
            if hts[-1] == NHT - 1:
                act_hidden_high(act, f, n, NHT - 1)

        def dve_x_low(dve, dst, high, n, high_done, done, bank=TB):
            for k in range(KD):
                dve.wait_ge(high_done, KD * n + k + 1)
                dve.tensor_tensor(dst[:, k, :], ps[:, bank + k, :], high[:, k, :].bitcast(F32), ALU.subtract)\
                   .then_inc(done, 1)

        def dve_hidden(dve, f, n, hts):
            for ht in hts:
                g, r = n * NHT + ht, ht % 2
                dve.wait_ge(silu_ready, g + 1)
                dve.wait_ge(lin_ready, g + 1)
                if later(g - 1):
                    dve.wait_ge(hl_ready, g - 1)
                dve.tensor_tensor(f.hid[:, r, :], ps[:, LIN[r], :], f.silu[:, r, :], ALU.mult).then_inc(hid_ready, 1)

        def dve_residual(dve, f, n, stored):
            for b in range(2):
                dve.wait_ge(y_ready, TPC * n + 2 * b + 2)
                if b == 0:
                    dve.wait_ge(xres_ready, n + 1)
                    if later(stored):
                        dve.wait_ge(xo_stored, stored)
                dve.tensor_tensor(f.xo[:, 2 * b:2 * b + 2, :], ps[:, YB + b, :].rearrange("p (j d) -> p j d", d=D),
                                  f.xres[:, 2 * b:2 * b + 2, :], ALU.add).then_inc(xo_ready, 1)

        def dve_keep_residual(dve, f, n):
            if later(2 * n):
                dve.wait_ge(xo_ready, 2 * n)
            dve.tensor_copy(f.xres[:], f.xin[:]).then_inc(xres_ready, 1)

        def pool_hidden_low(pool, f, n, hts):
            for ht in hts:
                g, r = n * NHT + ht, ht % 2
                pool.wait_ge(hh_ready, g + 1)
                pool.tensor_tensor(f.hl[:, ht, :], f.hid[:, r, :], f.hh[:, ht, :].bitcast(F32), ALU.subtract)\
                    .then_inc(hl_ready, 1)

        def rows(dram, c):
            return dram[bass.ts(c, CH), :].rearrange("(j p) d -> p j d", p=P)

        w1_loaded, w3_loaded, w2_loaded, wp_loaded = sem("w1_loaded"), sem("w3_loaded"), sem("w2_loaded"), sem("wp_loaded")
        had_loaded, ident_loaded, bias_loaded = sem("had_loaded"), sem("ident_loaded"), sem("bias_loaded")
        w13_h_ready, w13_l_ready, wp_h_ready, wp_l_ready = (
            sem("w13_h_ready"), sem("w13_l_ready"), sem("wp_h_ready"), sem("wp_l_ready"))
        fwht_step, w2x_h_ready, w2x_ready, had_ready = sem("fwht_step"), sem("w2x_h_ready"), sem("w2x_ready"), sem("had_ready")
        w2_ps_ready, w2_h_ready, w2_l_ready = sem("w2_ps_ready"), sem("w2_h_ready"), sem("w2_l_ready")
        mid_stats, mid_var, mid_rstd, x1n_ready = sem("mid_stats"), sem("mid_var"), sem("mid_rstd"), sem("x1n_ready")
        mid_seed, mid_newton = sem("mid_seed"), sem("mid_newton")
        x1T_ready, x1h_ready, x1l_ready = sem("x1T_ready"), sem("x1h_ready"), sem("x1l_ready")
        proj_ready, qb_ready, v_ready, v_kept, v_stored = (
            sem("proj_ready"), sem("qb_ready"), sem("v_ready"), sem("v_kept"), sem("v_stored"))
        table_loaded, swap_ready, sin_ready, cos_ready, rope_ready = (
            sem("table_loaded"), sem("swap_ready"), sem("sin_ready"), sem("cos_ready"), sem("rope_ready"))
        rope_h_ready, rope_l_ready = sem("rope_h_ready"), sem("rope_l_ready")
        rope_h_stored = [sem(f"rope_h_stored{j}") for j in range(4)]
        rope_l_stored = [sem(f"rope_l_stored{j}") for j in range(4)]
        ones_ready = sem("ones_ready")
        NPJ = 2 * KD
        PIECE_BANK = (GATE[0], LIN[0], GATE[1], LIN[1])
        f1, f3, mid = Buffers(), Buffers(), Buffers()
        for buffers, t in ((f1, 1), (f3, 3), (mid, "_mid")):
            ln_buffers(buffers, t)
        with ExitStack() as scope:
            input_buffers(f1, scope, 1)
            ffn_buffers(f1, scope, 1)
            cos_s, sin_s = sb("cos_s", [P, CH], F32, scope), sb("sin_s", [P, CH], F32, scope)
            with ExitStack() as weights:
                w1_raw = sb("w1_raw", [P, KD, HID], F32, weights)
                w3_raw = sb("w3_raw", [P, KD, HID], F32, weights)
                fa, fb = sb("fa", [P, NHT, D], F32, weights), sb("fb", [P, NHT, D], F32, weights)
                w2x_h, w2x_l = sb("w2x_h", [P, NHT, D], F32R, weights), sb("w2x_l", [P, NHT, D], F32R, weights)
                wp_raw = sb("wp_raw", [P, 4, KD, D], F32, weights)
                had_raw, had = sb("had_raw", [P, P], F32, weights), sb("had", [P, P], F32R, weights)
            vaug = sb("vaug", [P, TPC, NH, 32], F32, scope)
            x1n = sb("x1n", [P, TPC, D], F32, scope)
            x1h, x1l = sb("x1h", [P, KD, CH], F32R, scope), sb("x1l", [P, KD, CH], F32R, scope)
            qb = sb("qb", [P, 2, CH], F32, scope)
            swap = sb("swap", [P, 2, CH], F32, scope)
            qcos = sb("qcos", [P, 2, CH], F32, scope)
            rope = sb("rope", [P, 2, CH], F32, scope)
            rope_h, rope_l = sb("rope_h", [P, NPJ, CH], F32R, scope), sb("rope_l", [P, NPJ, CH], F32R, scope)

        q_loaded = [sem(f"q_loaded{a}") for a in range(3)]
        k_loaded = [sem(f"k_loaded{a}") for a in range(3)]
        vq_loaded = [sem(f"vq_loaded{a}") for a in range(3)]
        causal_loaded = sem("causal_loaded")
        clear_ready, ones_made, head_rows_stored = sem("clear_ready"), sem("ones_made"), sem("head_rows_stored")
        score_ready, max_ready, row_max_ready = sem("score_ready"), sem("max_ready"), sem("row_max_ready")
        negmax_loaded = [sem(f"negmax_loaded{r}") for r in range(2)]
        keyed_ready, prob_ready, masked_ready = sem("keyed_ready"), sem("prob_ready"), sem("masked_ready")
        pv_ready, att_ready, att_stored = sem("pv_ready"), sem("att_ready"), sem("att_stored")
        sums_loaded, rec_ready, rec_stored = sem("sums_loaded"), sem("rec_ready"), sem("rec_stored")
        KEYED, SCORE, ATT = 0, 3, 6
        STEPS = 4 * NB
        BLOCKS = (0, 4, 1, 5, 2, 6, 3, 7)
        PIECES = []
        for i in range(NB):
            w = P * (i + 1)
            if w <= CH:
                PIECES.append((i, 0, w, max(w, 256), True))
            else:
                first = 384 if w == 640 else CH
                PIECES.append((i, 0, first, first, False))
                PIECES.append((i, first, w - first, max(w - first, 256), True))
        NP = len(PIECES)
        ORDER = []
        for h in range(4):
            for k in range(NP):
                ORDER.append(("piece", h, k))
                if h and k == 2:
                    ORDER.append(("turn", h - 1, 0))
        ORDER.append(("turn", 3, 0))
        NO = len(ORDER)
        SHARE = (8, 6, 8, 6, 7, 5, 7, 4)
        STEP_PIECES = [(2 if S - BLOCKS[k // 4] * P > CH else 1) for k in range(STEPS)]
        PIECE_AT = [sum(STEP_PIECES[:k]) for k in range(STEPS + 1)]
        NK = PIECE_AT[STEPS]
        TURN_AT = [ORDER.index(("turn", h, 0)) for h in range(4)]
        qst, kst, vq = [None] * 3, [None] * 3, [None] * 3
        with ExitStack() as scope:
            def queries(a):
                qst[a] = [sb(f"qst{a}{g}", [P, S], F32R, scope) for g in range(2)]
            def keys(a):
                kst[a] = [sb(f"kst{a}{h}", [P, S], F32R, scope) for h in range(4)]
            def value_rows(a):
                vq[a] = sb(f"vq{a}", [P, NB, 4, 32], F32, scope)
            queries(1), keys(1), value_rows(1), value_rows(2)
            queries(0), keys(0), value_rows(0)
            queries(2), keys(2)
            prob = sb("prob", [P, 8, S], F32, scope)

        rec_loaded, att_loaded, bias_ready, norm_ready = sem("rec_loaded"), sem("att_loaded"), sem("bias_ready"), sem("norm_ready")
        ah_ready, al_ready, wo_ready, x2_ready = sem("ah_ready"), sem("al_ready"), sem("wo_ready"), sem("x2_ready")
        with ExitStack() as scope:
            input_buffers(f3, scope, 3)
            attn = sb("attn", [P, KD, CH], F32, scope)
            inv = sb("inv", [P, KD, CH], F32, scope)
            ah, al = sb("ah", [P, KD, CH], F32R, scope), sb("al", [P, KD, CH], F32R, scope)
            ffn_buffers(f3, scope, 3)

            def load_residual(sp, c):
                if later(c):
                    sp.wait_ge(xres_ready, NC + c)
                    sp.wait_ge(xn_ready, NC + c)
                sp.dma_start(f3.xin[:], rows(x1_d, c)).then_inc(xin_loaded, 16)

            def load_attention(sp, c):
                b, half = c // 2, c % 2
                if later(c):
                    sp.wait_ge(al_ready, KD * c)
                for k in range(KD):
                    sp.dma_start(attn[:, k, :], att_d[c, k * P:(k + 1) * P, :]).then_inc(att_loaded, 16)
                    sp.dma_start(inv[:, k, :],
                                 rec_d[bass.ds(4 * b + 2 * k, 2), :, bass.ts(half, CH)].rearrange("q h t -> (q h) t")
                                 .unsqueeze(1).broadcast_to([8, DH, CH])).then_inc(rec_loaded, 16)
            def project_attention(pe, c, bank=TB):
                pe.wait_ge(ah_ready, KD * c + KD)
                pe.wait_ge(al_ready, KD * c + KD)
                for j in range(TPC):
                    dst, cols = ps[:, bank + j // 2, (j % 2) * D:(j % 2 + 1) * D], slice(j * P, (j + 1) * P)
                    for k in range(KD):
                        pe.matmul(dst, ah[:, k, cols], wp_h[:, 3, k, :], start=(k == 0), stop=False)
                        pe.matmul(dst, ah[:, k, cols], wp_l[:, 3, k, :], start=False, stop=False)
                        ins = pe.matmul(dst, al[:, k, cols], wp_h[:, 3, k, :], start=False, stop=(k == KD - 1))
                    ins.then_inc(wo_ready, 1)

            def transpose_x2(pe, c, bank=TB):
                pe.wait_ge(xn_ready, NC + c + 1)
                pe_transpose(pe, f3.xn, xT_ready, bank)

            def act_split(act, c):
                for k in range(KD):
                    act.wait_ge(norm_ready, KD * c + k + 1)
                    if k == 0 and later(TPC * c):
                        act.wait_ge(wo_ready, TPC * c)
                    act.activation(ah[:, k, :], attn[:, k, :], ACT.Identity).then_inc(ah_ready, 1)

            def normalise(dve, c):
                dve.wait_ge(att_loaded, 16 * KD * (c + 1))
                dve.wait_ge(rec_loaded, 16 * KD * (c + 1))
                for k in range(KD):
                    dve.tensor_tensor(attn[:, k, :], attn[:, k, :], inv[:, k, :], ALU.mult).then_inc(norm_ready, 1)

            def attention_out(dve, c, bank=TB):
                for j in range(TPC):
                    dve.wait_ge(wo_ready, TPC * c + (j // 2) * 2 + 2)
                    dve.wait_ge(bias_ready, TPC * c + j + 1)
                    dve.tensor_tensor(f3.xin[:, j, :], ps[:, bank + j // 2, (j % 2) * D:(j % 2 + 1) * D],
                                      f3.xin[:, j, :], ALU.add).then_inc(x2_ready, 1)
                dve.wait_ge(x2_ready, TPC * c + TPC)
                ln_stats(dve, f3.xin, f3, NC + c, stats_ready, var_ready, seed_ready)

            def scale_x2(dve, c):
                dve.wait_ge(xT_ready, KD * (NC + c))
                ln_scale(dve, f3.xn, f3.xin, f3, NC + c, rstd_ready, xn_ready)

            def pool_split(pool, c):
                for k in range(KD):
                    pool.wait_ge(ah_ready, KD * c + k + 1)
                    pool.tensor_tensor(al[:, k, :], attn[:, k, :], ah[:, k, :].bitcast(F32), ALU.subtract)\
                        .then_inc(al_ready, 1)

            def add_bias(pool, c):
                pool.wait_ge(xin_loaded, 16 * (NC + c + 1))
                for j in range(TPC):
                    pool.tensor_tensor(f3.xin[:, j, :], f3.xin[:, j, :], bvo_s[:, 1, :], ALU.add).then_inc(bias_ready, 1)
            def store_att(sp, q, half):
                b, u = q // 4, q % 4
                sp.wait_ge(att_ready, 2 * q + half + 1)
                for h in range(4):
                    sp.dma_start(att_d[2 * b + half, bass.ds(64 * u + DH * h, DH), :],
                                 att[32 * h:32 * h + DH, half, :]).then_inc(att_stored, 16)
                    sp.dma_start(sums[32 * h + 16 * half:32 * h + 16 * half + 16, :],
                                 att[32 * h + DH:32 * h + DH + 1, half, :]).then_inc(sums_loaded, 16)

            def store_rec(sp, q):
                sp.wait_ge(rec_ready, q + 1)
                sp.dma_start(rec_d[q, :, :].rearrange("h (p n) -> (h p) n", n=32), rec[:])\
                  .then_inc(rec_stored, 16)

            def reciprocal(dve, q):
                dve.wait_ge(sums_loaded, 16 * 8 * (q + 1))
                if later(q):
                    dve.wait_ge(rec_stored, 16 * q)
                dve.reciprocal(rec[:], sums[:]).then_inc(rec_ready, 1)

            def clear_keys(pool, a, heads=range(4)):
                for h in heads:
                    if 4 * a + h:
                        pool.wait_ge(clear_ready, 4 * a + h)
                    pool.memset(kst[a][h][:].bitcast(F32), 0.0).then_inc(clear_ready, 1)

            def load_head_rows(sp, a):
                if a == 0:
                    sp.wait_ge(head_rows_stored, 16 * 4)
                sp.wait_ge(clear_ready, 4 * (a + 1))
                for h in range(4):
                    sp.dma_start(kst[a][h][96:98, :].bitcast(F32), head_d[h % 2]).then_inc(k_loaded[a], 16)

            def load_quad(sp, q, a):
                b, u = q // 4, q % 4
                if later(q - 2):
                    sp.wait_ge(pv_ready, NB * (q - 2))
                for part, row in ((0, 0), (1, 32), (0, 64)):
                    for g in range(2):
                        sp.dma_start(qst[a][g][row:row + 32, :].bitcast(F32).rearrange("r (u t) -> r u t", u=2),
                                     qk_d[part, 0, bass.ds(2 * b, 2), bass.ds(64 * u + 32 * g, 32), :]
                                     .rearrange("u r t -> r u t")).then_inc(q_loaded[a], 16)
                for part, row in ((0, 0), (0, 32), (1, 64)):
                    for h in range(4):
                        r = row + DH * (h % 2)
                        sp.dma_start(kst[a][h][r:r + DH, :].bitcast(F32).rearrange("r (u t) -> r u t", u=2),
                                     qk_d[part, 1, bass.ds(2 * b, 2), bass.ds(64 * u + DH * h, DH), :]
                                     .rearrange("u r t -> r u t")).then_inc(k_loaded[a], 16)
                sp.dma_start(vq[a][:].rearrange("p n h d -> p n (h d)"),
                             v_d[bass.ts(b, S), bass.ts(u, P)].rearrange("(n p) f -> p n f", p=P))\
                  .then_inc(vq_loaded[a], 16)

            def load_negmax(sp, q, a, heads):
                for h in heads:
                    sp.wait_ge(max_ready, NO * q + TURN_AT[h] + 1)
                    sp.dma_start(qst[a][h // 2][96 + h % 2:97 + h % 2, :].bitcast(F32),
                                 negmax[:, h % 2, :].bitcast(F32)).then_inc(negmax_loaded[h % 2], 16)

            def pe_first_pass(pe, q, a, j, n):
                kind, h, k = ORDER[n]
                s, bank = NO * q + n, SCORE + (NO * a + n) % 3
                if n == 0:
                    pe.wait_ge(q_loaded[a], 16 * 6 * (j + 1))
                    pe.wait_ge(k_loaded[a], 16 * (12 * (j + 1) + 4))
                if later(s - 2):
                    pe.wait_ge(max_ready, s - 2)
                if kind == "piece":
                    i, t0, _, cols, _ = PIECES[k]
                    pe.matmul(ps[:, bank, 0:cols], qst[a][h // 2][0:96, i * P:(i + 1) * P],
                              kst[a][h][0:96, t0:t0 + cols], start=True, stop=True).then_inc(score_ready, 1)
                else:
                    pe.wait_ge(row_max_ready, 4 * q + h + 1)
                    pe.transpose(ps[0:NB, bank, 0:P], part_max[:, h % 2, 0:NB], ident[:]).then_inc(score_ready, 1)

            def dve_first_pass(dve, q, a, n):
                kind, h, k = ORDER[n]
                ring = (NO * a + n) % 3
                s, bank, m = NO * q + n, SCORE + ring, part_max[:, h % 2, :]
                dve.wait_ge(score_ready, s + 1)
                if kind == "turn":
                    if later(2 * q + h // 2):
                        dve.wait_ge(negmax_loaded[h % 2], 16 * (2 * q + h // 2))
                    dve.tensor_scalar(negmax[:, h % 2, :], ps[0:NB, bank, 0:P], -1.0, None, ALU.mult)\
                       .then_inc(max_ready, 1)
                    return
                i, _, keys, _, diagonal = PIECES[k]
                to = m[:, i:i + 1] if i < 4 or not diagonal else m[:, 4 + i:5 + i]
                if diagonal:
                    dve.sem_inc(dve_passed)
                    dve.tensor_tensor_reduce(junk[:, ring, 0:keys], ps[:, bank, 0:keys], causal_s[:, CH - keys:CH],
                                             1.0, -3e38, ALU.add, ALU.max, to).then_inc(max_ready, 1)
                else:
                    dve.tensor_reduce(to, ps[:, bank, 0:keys], AX.X, ALU.max).then_inc(max_ready, 1)
                if k == NP - 1:
                    dve.wait_ge(max_ready, s + 1)
                    dve.tensor_tensor(m[:, 4:8], m[:, 4:8], m[:, 8:12], ALU.max).then_inc(row_max_ready, 1)

            with nc.Block() as block:
                @block.sync
                def _(sp):
                    def load_x(c):
                        if later(c):
                            sp.wait_ge(xres_ready, c)
                            sp.wait_ge(xn_ready, c)
                        sp.dma_start(f1.xin[:], rows(x, c)).then_inc(xin_loaded, 16)

                    def load_tables(c):
                        if later(NPJ * c):
                            sp.wait_ge(rope_ready, NPJ * c)
                        sp.dma_start(cos_s[:], cos_t[:, bass.ts(c % 2, CH)]).then_inc(table_loaded, 16)
                        sp.dma_start(sin_s[:], sin_t[:, bass.ts(c % 2, CH)]).then_inc(table_loaded, 16)

                    def store_projections(c):
                        for j in range(NPJ):
                            m = NPJ * c + j
                            which, e = j // KD, j % KD
                            sp.wait_ge(rope_h_ready, m + 1)
                            sp.dma_start(qk_d[0, which, c, e * P:(e + 1) * P, :], rope_h[:, j, :].bitcast(F32))\
                              .then_inc(rope_h_stored[j], 16)
                            sp.wait_ge(rope_l_ready, m + 1)
                            sp.dma_start(qk_d[1, which, c, e * P:(e + 1) * P, :], rope_l[:, j, :].bitcast(F32))\
                              .then_inc(rope_l_stored[j], 16)
                        sp.wait_ge(v_kept, TPC * c + TPC)
                        sp.dma_start(rows(v_d, c), vaug[:].rearrange("p j h d -> p j (h d)")).then_inc(v_stored, 16)

                    def store_x1(c):
                        sp.wait_ge(xo_ready, 2 * c + 2)
                        sp.dma_start(rows(x1_d, c), f1.xo[:]).then_inc(xo_stored, 16)

                    load_x(0)
                    sp.dma_start(w1_raw[:], w1t.rearrange("(k p) h -> p k h", p=P)).then_inc(w1_loaded, 16)
                    sp.dma_start(w3_raw[:], w3t.rearrange("(k p) h -> p k h", p=P)).then_inc(w3_loaded, 16)
                    sp.dma_start(ident[:], identity).then_inc(ident_loaded, 16)
                    sp.dma_start(fa[:], w2t.rearrange("(c p) d -> p c d", p=P)).then_inc(w2_loaded, 16)
                    sp.dma_start(had_raw[:], hadamard).then_inc(had_loaded, 16)
                    sp.dma_start(wp_raw[:], wqkvo.rearrange("w (k p) e -> p w k e", p=P)).then_inc(wp_loaded, 16)
                    sp.dma_start(bqk_s[:], bqk).then_inc(bias_loaded, 16)
                    sp.dma_start(bvo_s[:], bvo).then_inc(bias_loaded, 16)
                    sp.dma_start(causal_s[:], causal).then_inc(causal_loaded, 16)
                    sp.wait_ge(ones_made, 2)
                    ones, zeros = (junk[r:r + 1, 0:2, :].rearrange("r b n -> r (b n)") for r in range(2))
                    for h in range(2):
                        for r in range(2):
                            sp.dma_start(head_d[h, r:r + 1], ones if r == h else zeros).then_inc(head_rows_stored, 16)
                    load_x(1)
                    store_x1(0)

                    def steady(c):
                        load_x(c + 1)
                        load_tables(c - 1)
                        store_projections(c - 1)
                        store_x1(c)

                    steady(1)
                    with sp.Fori(2, NC - 1) as c:
                        steady(c)
                    load_tables(NC - 2)
                    store_projections(NC - 2)
                    store_x1(NC - 1)
                    load_tables(NC - 1)
                    for j in range(NPJ):
                        sp.wait_ge(rope_h_stored[j], 16 * (NC - 1))
                        sp.wait_ge(rope_l_stored[j], 16 * (NC - 1))
                    sp.wait_ge(v_stored, 16 * (NC - 1))
                    for a in range(2):
                        load_head_rows(sp, a)
                        load_quad(sp, a, a)
                    store_projections(NC - 1)
                    load_negmax(sp, 0, 0, range(3))
                    for j in range(NPJ):
                        sp.wait_ge(rope_h_stored[j], 16 * NC)
                        sp.wait_ge(rope_l_stored[j], 16 * NC)
                    sp.wait_ge(v_stored, 16 * NC)
                    sp.wait_ge(xo_stored, 16 * NC)

                @block.tensor
                def _(pe):
                    def transpose_x(c):
                        pe.wait_ge(xn_ready, c + 1)
                        if later(TPC * (c - 1)):
                            pe.wait_ge(v_kept, TPC * (c - 1))
                        pe_transpose(pe, f1.xn, xT_ready)

                    def transpose_x1(c):
                        pe.wait_ge(x1n_ready, c + 1)
                        pe_transpose(pe, x1n, x1T_ready)

                    def project(c, silu_before, hid_before):
                        pe.wait_ge(x1h_ready, KD * c + KD)
                        pe.wait_ge(x1l_ready, KD * c + KD)
                        for j in range(NPJ):
                            which, e = j // KD, j % KD
                            bank, cols = PIECE_BANK[j], slice(e * P, (e + 1) * P)
                            if j % 2 == 0:
                                pe.wait_ge(silu_ready, silu_before - 1 + j // 2)
                            else:
                                pe.wait_ge(hid_ready, hid_before - 1 + j // 2)
                            for k in range(KD):
                                pe.matmul(ps[:, bank, :], wp_h[:, which, k, cols], x1h[:, k, :], start=(k == 0), stop=False)
                                pe.matmul(ps[:, bank, :], wp_h[:, which, k, cols], x1l[:, k, :], start=False, stop=False)
                                ins = pe.matmul(ps[:, bank, :], wp_l[:, which, k, cols], x1h[:, k, :],
                                                start=False, stop=(k == KD - 1))
                            ins.then_inc(proj_ready, 1)
                        for j in range(TPC):
                            dst, cols = ps[:, TB + j // 2, (j % 2) * D:(j % 2 + 1) * D], slice(j * P, (j + 1) * P)
                            for k in range(KD):
                                pe.matmul(dst, x1h[:, k, cols], wp_h[:, 2, k, :], start=(k == 0), stop=False)
                                pe.matmul(dst, x1h[:, k, cols], wp_l[:, 2, k, :], start=False, stop=False)
                                ins = pe.matmul(dst, x1l[:, k, cols], wp_h[:, 2, k, :], start=False, stop=(k == KD - 1))
                            ins.then_inc(v_ready, 1)

                    def transform_w2():
                        pe.wait_ge(had_ready, 1)
                        pe.wait_ge(w2x_ready, 1)
                        for c in range(NHT):
                            dst = ps[:, YB + c // 2, (c % 2) * D:(c % 2 + 1) * D]
                            pe.matmul(dst, had[:], w2x_h[:, c, :], start=True, stop=False)
                            pe.matmul(dst, had[:], w2x_l[:, c, :], start=False, stop=True).then_inc(w2_ps_ready, 1)

                    pe.wait_ge(ident_loaded, 16)
                    transpose_x(0)
                    pe.wait_ge(w13_h_ready, 2)
                    pe.wait_ge(w13_l_ready, 2)
                    pe_up(pe, f1, 0, range(5))
                    transform_w2()
                    pe_up(pe, f1, 0, range(5, NHT))
                    pe.wait_ge(w2_h_ready, 1)
                    pe.wait_ge(w2_l_ready, 1)
                    pe_down(pe, f1, 0, (0, 1))
                    transpose_x(1)
                    pe_down(pe, f1, 0, (2, 3))

                    def steady(c):
                        pe_up(pe, f1, c, range(6), banks_free=(qb_ready, NPJ * (c - 1)))
                        transpose_x1(c - 1)
                        pe_up(pe, f1, c, (6, 7))
                        project(c - 1, NHT * c + NHT, NHT * c + NHT)

                    def down(c):
                        pe_down(pe, f1, c, (0, 1, 2))
                        transpose_x(c + 1)
                        pe_down(pe, f1, c, (3,))

                    pe.wait_ge(wp_h_ready, 1)
                    pe.wait_ge(wp_l_ready, 1)
                    steady(1)
                    down(1)
                    with pe.Fori(2, NC - 1) as c:
                        steady(c)
                        down(c)
                    steady(NC - 1)
                    pe_down(pe, f1, NC - 1, range(TPC))
                    pe.wait_ge(v_kept, TPC * (NC - 1))
                    transpose_x1(NC - 1)
                    pe.wait_ge(qb_ready, NPJ * (NC - 1))
                    project(NC - 1, NHT * NC, NHT * NC)
                    pe.wait_ge(qb_ready, NPJ * NC)
                    for n in range(NO - 1):
                        pe_first_pass(pe, 0, 0, 0, n)

                @block.scalar
                def _(act):
                    def biased(c, j):
                        m, r = NPJ * c + j, j % 2
                        act.wait_ge(proj_ready, m + 1)
                        if later(m - 1):
                            act.wait_ge(swap_ready, m - 1)
                            act.wait_ge(cos_ready, m - 1)
                        act.activation(qb[:, r, :], ps[:, PIECE_BANK[j], :], ACT.Identity,
                                       bias=bqk_s[:, j // KD, j % KD:j % KD + 1]).then_inc(qb_ready, 1)

                    def rope_high(c, j):
                        m, r = NPJ * c + j, j % 2
                        act.wait_ge(rope_ready, m + 1)
                        if later(16 * c):
                            act.wait_ge(rope_h_stored[j], 16 * c)
                        act.activation(rope_h[:, j, :], rope[:, r, :], ACT.Identity).then_inc(rope_h_ready, 1)

                    def projections(c):
                        biased(c, 0)
                        for j in range(1, NPJ):
                            biased(c, j)
                            rope_high(c, j - 1)
                        rope_high(c, NPJ - 1)

                    for high, raw, loaded in ((w1_h, w1_raw, w1_loaded), (w3_h, w3_raw, w3_loaded)):
                        act.wait_ge(loaded, 16)
                        act.activation(high[:], raw[:], ACT.Identity).then_inc(w13_h_ready, 1)
                    act_x_high(act, f1.xh, 0, xT_ready, xh_ready)
                    act.wait_ge(had_loaded, 16)
                    act.activation(had[:], had_raw[:], ACT.Identity).then_inc(had_ready, 1)
                    act_up(act, f1, 0, range(4))
                    act.wait_ge(fwht_step, 6)
                    act.activation(w2x_h[:], fb[:], ACT.Identity).then_inc(w2x_h_ready, 1)
                    act_up(act, f1, 0, range(4, 7))
                    act.wait_ge(w2_ps_ready, NHT)
                    act.activation(w2_h[:], ps[:, YB:YB + 4, :].rearrange("p b (c d) -> p (b c) d", d=D), ACT.Identity,
                                   scale=0.5 / 32.0).then_inc(w2_h_ready, 1)
                    act_up(act, f1, 0, (7,))
                    act.wait_ge(wp_loaded, 16)
                    act.activation(wp_h[:], wp_raw[:], ACT.Identity).then_inc(wp_h_ready, 1)
                    act_x_high(act, f1.xh, 1, xT_ready, xh_ready)
                    act.wait_ge(bias_loaded, 32)

                    def steady(c):
                        act_up(act, f1, c, range(6))
                        act_x_high(act, x1h, c - 1, x1T_ready, x1h_ready)
                        act_up(act, f1, c, (6, 7))
                        projections(c - 1)

                    steady(1)
                    act_x_high(act, f1.xh, 2, xT_ready, xh_ready)
                    with act.Fori(2, NC - 1) as c:
                        steady(c)
                        act_x_high(act, f1.xh, c + 1, xT_ready, xh_ready)
                    steady(NC - 1)
                    act_x_high(act, x1h, NC - 1, x1T_ready, x1h_ready)
                    projections(NC - 1)

                @block.vector
                def _(dve):
                    def norm_in(c):
                        dve.wait_ge(xin_loaded, 16 * c + 16)
                        ln_stats(dve, f1.xin, f1, c, stats_ready, var_ready, seed_ready)

                    def scale_in(c):
                        if later(KD * c):
                            dve.wait_ge(xT_ready, KD * c)
                        ln_scale(dve, f1.xn, f1.xin, f1, c, rstd_ready, xn_ready)

                    def norm_mid(c):
                        dve.wait_ge(xo_ready, 2 * c + 2)
                        ln_stats(dve, f1.xo, mid, c, mid_stats, mid_var, mid_seed)

                    def scale_mid(c):
                        if later(KD * c):
                            dve.wait_ge(x1T_ready, KD * c)
                        ln_scale(dve, x1n, f1.xo, mid, c, mid_rstd, x1n_ready)

                    def swap_rows(c, j):
                        m, r = NPJ * c + j, j % 2
                        dve.wait_ge(qb_ready, m + 1)
                        if later(m - 1):
                            dve.wait_ge(rope_ready, m - 1)
                        dve.sem_inc(dve_passed)
                        dve.stream_shuffle(swap[:, r, :], qb[:, r, :], [i ^ 1 for i in range(32)]).then_inc(swap_ready, 1)

                    def rotate(c, j):
                        m, r = NPJ * c + j, j % 2
                        dve.wait_ge(swap_ready, m + 1)
                        if j == 0:
                            dve.wait_ge(table_loaded, 32 * c + 32)
                        dve.tensor_tensor(swap[:, r, :], swap[:, r, :], sin_s[:], ALU.mult).then_inc(sin_ready, 1)
                        dve.wait_ge(sin_ready, m + 1)
                        dve.wait_ge(cos_ready, m + 1)
                        if later(m - 1):
                            dve.wait_ge(rope_l_ready, m - 1)
                        dve.tensor_tensor(rope[:, r, :], swap[:, r, :], qcos[:, r, :], ALU.add).then_inc(rope_ready, 1)

                    def projections(c):
                        swap_rows(c, 0)
                        for j in range(1, NPJ):
                            swap_rows(c, j)
                            rotate(c, j - 1)
                        rotate(c, NPJ - 1)
                        for j in range(TPC):
                            dve.wait_ge(v_ready, TPC * c + (j // 2) * 2 + 2)
                            if j == 0 and later(16 * c):
                                dve.wait_ge(v_stored, 16 * c)
                            dve.tensor_tensor(vaug[:, j, :, 0:DH],
                                              ps[:, TB + j // 2, (j % 2) * D:(j % 2 + 1) * D].rearrange("p (h d) -> p h d", d=DH),
                                              bvo_s[:, 0, :].rearrange("p (h d) -> p h d", d=DH), ALU.add).then_inc(v_kept, 1)

                    def weights_low(n, low, high, raw):
                        dve.wait_ge(w13_h_ready, n + 1)
                        dve.tensor_tensor(low[:], raw[:], high[:].bitcast(F32), ALU.subtract).then_inc(w13_l_ready, 1)

                    def butterflies(n, src, dst, half):
                        s = src[:].rearrange("p (g two h) d -> p g two (h d)", two=2, h=half)
                        d = dst[:].rearrange("p (g two h) d -> p g two (h d)", two=2, h=half)
                        if n:
                            dve.wait_ge(fwht_step, 2 * n)
                        dve.tensor_tensor(d[:, :, 0], s[:, :, 0], s[:, :, 1], ALU.add).then_inc(fwht_step, 1)
                        dve.tensor_tensor(d[:, :, 1], s[:, :, 0], s[:, :, 1], ALU.subtract).then_inc(fwht_step, 1)

                    dve.memset(junk[0:2], 0.0).then_inc(ones_made, 1)
                    dve.wait_ge(ones_made, 1)
                    dve.memset(junk[0:1], 1.0).then_inc(ones_made, 1)
                    norm_in(0)
                    weights_low(0, w1_l, w1_h, w1_raw)
                    scale_in(0)
                    weights_low(1, w3_l, w3_h, w3_raw)
                    dve_x_low(dve, f1.xl, f1.xh, 0, xh_ready, xl_ready)
                    dve_keep_residual(dve, f1, 0)
                    dve.wait_ge(w2_loaded, 16)
                    butterflies(0, fa, fb, 1)
                    dve_hidden(dve, f1, 0, (0,))
                    butterflies(1, fb, fa, 2)
                    dve_hidden(dve, f1, 0, (1,))
                    butterflies(2, fa, fb, 4)
                    dve_hidden(dve, f1, 0, (2, 3))
                    dve.wait_ge(w2x_h_ready, 1)
                    dve.tensor_tensor(w2x_l[:], fb[:], w2x_h[:].bitcast(F32), ALU.subtract).then_inc(w2x_ready, 1)
                    norm_in(1)
                    dve_hidden(dve, f1, 0, (4,))
                    scale_in(1)
                    dve_hidden(dve, f1, 0, (5, 6))
                    dve.wait_ge(w2_h_ready, 1)
                    dve.scalar_tensor_tensor(w2_l[:].rearrange("p c d -> p (c d)"),
                                             ps[:, YB:YB + 4, :].rearrange("p b n -> p (b n)"), 0.5 / 32.0,
                                             w2_h[:].bitcast(F32).rearrange("p c d -> p (c d)"),
                                             ALU.mult, ALU.subtract).then_inc(w2_l_ready, 1)
                    dve_hidden(dve, f1, 0, (7,))
                    dve.memset(vaug[:], 1.0).then_inc(ones_ready, 1)
                    dve.wait_ge(ones_ready, 1)
                    dve.wait_ge(bias_loaded, 32)
                    dve_x_low(dve, f1.xl, f1.xh, 1, xh_ready, xl_ready)
                    dve_residual(dve, f1, 0, 0)
                    dve_keep_residual(dve, f1, 1)
                    norm_mid(0)

                    def steady(c, last):
                        dve_hidden(dve, f1, c, range(2))
                        scale_mid(c - 1)
                        dve_hidden(dve, f1, c, (2,))
                        if not last:
                            norm_in(c + 1)
                        dve_hidden(dve, f1, c, (3,))
                        if not last:
                            scale_in(c + 1)
                        dve_hidden(dve, f1, c, (4, 5))
                        dve_x_low(dve, x1l, x1h, c - 1, x1h_ready, x1l_ready)
                        dve_hidden(dve, f1, c, (6, 7))
                        projections(c - 1)
                        if not last:
                            dve_x_low(dve, f1.xl, f1.xh, c + 1, xh_ready, xl_ready)
                        dve_residual(dve, f1, c, 16 * c)
                        if not last:
                            dve_keep_residual(dve, f1, c + 1)
                        norm_mid(c)

                    steady(1, False)
                    with dve.Fori(2, NC - 1) as c:
                        steady(c, False)
                    steady(NC - 1, True)
                    scale_mid(NC - 1)
                    dve_x_low(dve, x1l, x1h, NC - 1, x1h_ready, x1l_ready)
                    projections(NC - 1)
                    dve.wait_ge(causal_loaded, 16)
                    dve.wait_ge(head_rows_stored, 16 * 4)
                    for n in range(NO - 1):
                        dve_first_pass(dve, 0, 0, n)

                @block.gpsimd
                def _(pool):
                    def times_cos(c, j):
                        m, r = NPJ * c + j, j % 2
                        if j == 0:
                            pool.wait_ge(table_loaded, 32 * c + 32)
                        pool.wait_ge(qb_ready, m + 1)
                        if later(m - 1):
                            pool.wait_ge(rope_ready, m - 1)
                        pool.tensor_tensor(qcos[:, r, :], qb[:, r, :], cos_s[:], ALU.mult).then_inc(cos_ready, 1)

                    def rope_low(c, j):
                        m, r = NPJ * c + j, j % 2
                        pool.wait_ge(rope_h_ready, m + 1)
                        if later(16 * c):
                            pool.wait_ge(rope_l_stored[j], 16 * c)
                        pool.tensor_tensor(rope_l[:, j, :], rope[:, r, :], rope_h[:, j, :].bitcast(F32), ALU.subtract)\
                            .then_inc(rope_l_ready, 1)

                    def projections(c):
                        times_cos(c, 0)
                        for j in range(1, NPJ):
                            times_cos(c, j)
                            rope_low(c, j - 1)
                        rope_low(c, NPJ - 1)

                    ln_rstd(pool, f1, 0, seed_ready, newton_step, rstd_ready)
                    pool_hidden_low(pool, f1, 0, range(4))
                    ln_rstd(pool, f1, 1, seed_ready, newton_step, rstd_ready)
                    pool_hidden_low(pool, f1, 0, range(4, NHT))
                    pool.wait_ge(wp_h_ready, 1)
                    pool.tensor_tensor(wp_l[:], wp_raw[:], wp_h[:].bitcast(F32), ALU.subtract).then_inc(wp_l_ready, 1)
                    ln_rstd(pool, mid, 0, mid_seed, mid_newton, mid_rstd)

                    def steady(c, last):
                        pool_hidden_low(pool, f1, c, range(3))
                        if not last:
                            ln_rstd(pool, f1, c + 1, seed_ready, newton_step, rstd_ready)
                        pool_hidden_low(pool, f1, c, range(3, NHT))
                        projections(c - 1)
                        if last:
                            pool.wait_ge(xo_ready, 2 * NC)
                            clear_keys(pool, 0, (0, 1))
                            pool.wait_ge(clear_ready, 2)
                        ln_rstd(pool, mid, c, mid_seed, mid_newton, mid_rstd)

                    steady(1, False)
                    with pool.Fori(2, NC - 1) as c:
                        steady(c, False)
                    steady(NC - 1, True)
                    clear_keys(pool, 0, (2, 3))
                    clear_keys(pool, 1)
                    pool.wait_ge(clear_ready, 4 * 2)
                    projections(NC - 1)

            with nc.Block() as block:
                @block.sync
                def _(sp):
                    load_negmax(sp, 0, 0, (3,))
                    load_head_rows(sp, 2)

                    def slot(q, a, last=0):
                        if last < 1:
                            load_quad(sp, q + 2, (a + 2) % 3)
                        if last < 2:
                            load_negmax(sp, q + 1, (a + 1) % 3, range(3))
                        if last == 2:
                            sp.wait_ge(pv_ready, NB * q)
                            load_attention(sp, 0)
                            load_residual(sp, 0)
                        if later(q):
                            store_rec(sp, q - 1)
                        if last < 2:
                            load_negmax(sp, q + 1, (a + 1) % 3, (3,))
                            store_att(sp, q, 0)
                            store_att(sp, q, 1)

                    for q in range(3):
                        slot(q, q)
                    with sp.Fori(1, QUADS // 3 - 1) as j:
                        for a in range(3):
                            slot(3 * j + a, a)
                    slot(QUADS - 4, 0)
                    slot(QUADS - 3, 1)
                    slot(QUADS - 2, 2, last=1)
                    slot(QUADS - 1, 0, last=2)
                    load_attention(sp, 1)

                @block.tensor
                def _(pe):
                    def keyed(q, a, step, h, b):
                        i = BLOCKS[step]
                        if step == 0 and b == 0:
                            pe.wait_ge(negmax_loaded[h % 2], 16 * (2 * q + h // 2 + 1))
                        w = S - i * P
                        rows_used = 97 + h % 2
                        lhs = kst[a][h][0:rows_used, i * P:(i + 1) * P]
                        n = STEP_PIECES[4 * step + h]
                        at = PIECE_AT[4 * step + h] + b
                        if later(NK * q + at - 2):
                            pe.wait_ge(prob_ready, NK * q + at - 2)
                        cols = w // n
                        s0 = i * P + b * cols
                        if cols < 256:
                            s0, cols = S - 256, 256
                        pe.matmul(ps[:, KEYED + at % 3, 0:cols], lhs, qst[a][h // 2][0:rows_used, s0:s0 + cols],
                                  start=True, stop=True).then_inc(keyed_ready, 1)

                    def values(q, a, j, step, halves):
                        i = BLOCKS[step]
                        if step == 0 and 0 in halves:
                            pe.wait_ge(vq_loaded[a], 16 * (j + 1))
                        pe.wait_ge(prob_ready, NK * q + PIECE_AT[4 * step + 4])
                        pe.wait_ge(masked_ready, STEPS * q + 4 * step + 4)
                        for half in halves:
                            if half * CH + CH <= i * P:
                                continue
                            if step == 0 and later(2 * q - 1 + half):
                                pe.wait_ge(att_ready, 2 * q - 1 + half)
                            first = max(i * P, half * CH)
                            for h in range(4):
                                ins = pe.matmul(ps[32 * h:32 * h + 32, ATT + half, first - half * CH:CH],
                                                vq[a][:, i, h, :],
                                                prob[:, 4 * (step % 2) + h, first - i * P:half * CH + CH - i * P],
                                                start=(step == 0), stop=(i == 4 * half + 3), tile_position=(0, 32 * h))
                        if 1 in halves:
                            ins.then_inc(pv_ready, 1)

                    def slot(q, a, j, more=True):
                        n = 0
                        for k in range(STEPS):
                            step, h = k // 4, k % 4
                            if not more and k == 4 * 4:
                                pe.wait_ge(max_ready, NO * QUADS)
                                project_attention(pe, 0, SCORE)
                            for b in range(STEP_PIECES[k]):
                                keyed(q, a, step, h, b)
                                if k == 0 and b == 0:
                                    pe_first_pass(pe, q, a, j, NO - 1)
                                m, pieces = h * STEP_PIECES[k] + b, 4 * STEP_PIECES[k]
                                for _ in range(SHARE[step] * (m + 1) // pieces - SHARE[step] * m // pieces if more else 0):
                                    pe_first_pass(pe, q + 1, (a + 1) % 3, j + (a + 1) // 3, n)
                                    n += 1
                            if step and h == 1:
                                values(q, a, j, step - 1, (0,))
                            if step and h == 2:
                                values(q, a, j, step - 1, (1,))
                        values(q, a, j, NB - 1, (0, 1))

                    for q in range(3):
                        slot(q, q, 0)
                    with pe.Fori(1, QUADS // 3) as j:
                        for a in range(3):
                            slot(3 * j + a, a, j)
                    slot(QUADS - 1, 0, QUADS // 3, more=False)
                    transpose_x2(pe, 0, SCORE)

                @block.scalar
                def _(act):
                    def exponential(q, step, h):
                        i = BLOCKS[step]
                        if h == 0 and later(NB * q + step - 1):
                            act.wait_ge(pv_ready, NB * q + step - 1)
                        w = S - i * P
                        n = STEP_PIECES[4 * step + h]
                        skip = 256 - w if w < 256 else 0
                        cols = w // n
                        for b in range(n):
                            at = PIECE_AT[4 * step + h] + b
                            act.wait_ge(keyed_ready, NK * q + at + 1)
                            act.activation(prob[:, 4 * (step % 2) + h, b * cols:(b + 1) * cols],
                                           ps[:, KEYED + at % 3, skip:skip + cols], ACT.Exp, scale=SCALE)\
                               .then_inc(prob_ready, 1)

                    def evacuate(q, half):
                        act.wait_ge(pv_ready, NB * q + BLOCKS.index(4 * half + 3) + 1)
                        if later(q):
                            act.wait_ge(att_stored, 16 * 8 * q)
                            act.wait_ge(sums_loaded, 16 * 8 * q)
                        act.activation(att[:, half, :], ps[:, ATT + half, :], ACT.Identity).then_inc(att_ready, 1)

                    def slot(q, last=False):
                        for k in range(STEPS):
                            if last and k == 4 * 3:
                                act_split(act, 0)
                            if k == 2 and later(q):
                                evacuate(q - 1, 1)
                            exponential(q, k // 4, k % 4)
                        evacuate(q, 0)

                    slot(0)
                    slot(1)
                    with act.Fori(1, QUADS // 2 - 1) as j:
                        slot(2 * j)
                        slot(2 * j + 1)
                    slot(QUADS - 2)
                    slot(QUADS - 1, last=True)
                    evacuate(QUADS - 1, 1)
                    act_x_high(act, f3.xh, NC, xT_ready, xh_ready, SCORE)

                @block.vector
                def _(dve):
                    def slot(q, a):
                        dve_first_pass(dve, q, a, NO - 1)
                        for n in range(NO // 2):
                            dve_first_pass(dve, q + 1, (a + 1) % 3, n)
                        if later(q):
                            reciprocal(dve, q - 1)
                        for n in range(NO // 2, NO - 1):
                            dve_first_pass(dve, q + 1, (a + 1) % 3, n)

                    for q in range(3):
                        slot(q, q)
                    with dve.Fori(1, QUADS // 3) as j:
                        for a in range(3):
                            slot(3 * j + a, a)
                    dve_first_pass(dve, QUADS - 1, 0, NO - 1)
                    reciprocal(dve, QUADS - 2)
                    normalise(dve, 0)
                    attention_out(dve, 0, SCORE)
                    scale_x2(dve, 0)
                    dve_x_low(dve, f3.xl, f3.xh, NC, xh_ready, xl_ready, SCORE)

                @block.gpsimd
                def _(pool):
                    clear_keys(pool, 2)
                    pool.wait_ge(clear_ready, 4 * 3)

                    def mask(q, step):
                        for h in range(4):
                            pool.wait_ge(prob_ready, NK * q + PIECE_AT[4 * step + h] + 1)
                            pool.sem_inc(pool_passed)
                            block_ = prob[:, 4 * (step % 2) + h, 0:P]
                            pool.affine_select(out=block_, in_=block_, compare_op=ALU.is_ge, fill=0.0, base=0,
                                               pattern=[[1, P]], channel_multiplier=-1).then_inc(masked_ready, 1)

                    with pool.Fori(0, QUADS - 1) as q:
                        for step in range(NB):
                            mask(q, step)
                    for step in range(NB):
                        mask(QUADS - 1, step)
                        if step == 2:
                            pool_split(pool, 0)
                        if step == 3:
                            add_bias(pool, 0)
                        if step == 6:
                            ln_rstd(pool, f3, NC, seed_ready, newton_step, rstd_ready)

            with nc.Block() as block:
                @block.sync
                def _(sp):
                    def store(c):
                        sp.wait_ge(xo_ready, 2 * (NC + c) + 2)
                        sp.dma_start(rows(out, c), f3.xo[:]).then_inc(xo_stored, 16)

                    load_residual(sp, 1)
                    store_att(sp, QUADS - 1, 0)
                    store_att(sp, QUADS - 1, 1)
                    store_rec(sp, QUADS - 1)
                    sp.wait_ge(att_stored, 16 * 8 * QUADS)
                    sp.wait_ge(rec_stored, 16 * QUADS)
                    load_attention(sp, 2)
                    store(0)
                    with sp.Fori(1, NC - 2) as c:
                        load_residual(sp, c + 1)
                        load_attention(sp, c + 2)
                        store(c)
                    load_residual(sp, NC - 1)
                    store(NC - 2)
                    store(NC - 1)
                    sp.wait_ge(xo_stored, 16 * 2 * NC)

                @block.tensor
                def _(pe):
                    with pe.Fori(0, NC - 1) as c:
                        pe_up(pe, f3, NC + c, range(4))
                        project_attention(pe, c + 1)
                        pe_up(pe, f3, NC + c, range(4, NHT))
                        transpose_x2(pe, c + 1)
                        pe_down(pe, f3, NC + c, range(TPC))
                    pe_up(pe, f3, 2 * NC - 1, range(NHT))
                    pe_down(pe, f3, 2 * NC - 1, range(TPC))

                @block.scalar
                def _(act):
                    with act.Fori(0, NC - 1) as c:
                        act_up(act, f3, NC + c, (0, 1))
                        act_split(act, c + 1)
                        act_up(act, f3, NC + c, range(2, NHT))
                        act_x_high(act, f3.xh, NC + c + 1, xT_ready, xh_ready)
                    act_up(act, f3, 2 * NC - 1, range(NHT))

                @block.vector
                def _(dve):
                    def steady(c, first=False):
                        n = NC + c
                        dve_hidden(dve, f3, n, (0,))
                        normalise(dve, c + 1)
                        dve_hidden(dve, f3, n, range(1, 4))
                        if first:
                            reciprocal(dve, QUADS - 1)
                        attention_out(dve, c + 1)
                        dve_hidden(dve, f3, n, (4, 5))
                        scale_x2(dve, c + 1)
                        dve_hidden(dve, f3, n, (6, 7))
                        dve_x_low(dve, f3.xl, f3.xh, n + 1, xh_ready, xl_ready)
                        dve_residual(dve, f3, n, 16 * n)
                        dve_keep_residual(dve, f3, n + 1)

                    dve_keep_residual(dve, f3, NC)
                    steady(0, first=True)
                    with dve.Fori(1, NC - 1) as c:
                        steady(c)
                    dve_hidden(dve, f3, 2 * NC - 1, range(NHT))
                    dve_residual(dve, f3, 2 * NC - 1, 16 * (2 * NC - 1))

                @block.gpsimd
                def _(pool):
                    with pool.Fori(0, NC - 1) as c:
                        pool_hidden_low(pool, f3, NC + c, (0,))
                        pool_split(pool, c + 1)
                        add_bias(pool, c + 1)
                        pool_hidden_low(pool, f3, NC + c, range(1, 4))
                        ln_rstd(pool, f3, NC + c + 1, seed_ready, newton_step, rstd_ready)
                        pool_hidden_low(pool, f3, NC + c, range(4, NHT))
                    pool_hidden_low(pool, f3, 2 * NC - 1, range(NHT))


def rotary_tables():
    pos = np.arange(S, dtype=np.float32)
    theta = np.power(np.float32(10000.0), -np.arange(0, DH, 2, dtype=np.float32) / np.float32(DH)).astype(np.float32)
    angle = pos[None, :] * np.repeat(theta, 2)[:, None]
    sign = np.where(np.arange(DH) % 2 == 0, -1.0, 1.0).astype(np.float32)[:, None]
    return np.tile(np.cos(angle), (P // DH, 1)), np.tile(np.sin(angle) * sign, (P // DH, 1))


def hadamard_matrix(n):
    h = np.ones((1, 1), np.float32)
    while h.shape[0] < n:
        h = np.block([[h, h], [h, -h]])
    return h.astype(np.float32)


def kernel(**inputs):
    import concourse.bacc as bacc
    from concourse.bass_utils import run_bass_kernel_spmd

    a = {k: np.asarray(v) for k, v in inputs.items()}
    c = np.ascontiguousarray
    cos, sin = rotary_tables()
    causal = np.zeros((P, CH), np.float32)
    causal[:, CH - P:] = np.where(np.arange(P)[None, :] > np.arange(P)[:, None], NEG, 0.0)
    arrays = {
        "x": c(a["L0_attn_x"].reshape(TOK, D)),
        "w1t": c(a["L0_ffn_W1"].T), "w3t": c(a["L0_ffn_W3"].T), "w2t": c(a["L0_ffn_W2"].T),
        "wqkvo": np.stack([a["L0_attn_Wq"], a["L0_attn_Wk"], a["L0_attn_Wv"], a["L0_attn_Wo"]]),
        "bqk": c(np.stack([a["L0_attn_bq"], a["L0_attn_bk"]]).reshape(2, KD, P).transpose(2, 0, 1)),
        "bvo": c(np.broadcast_to(np.stack([a["L0_attn_bv"], a["L0_attn_bo"]]), (P, 2, D))),
        "cos_t": c(cos.astype(np.float32)), "sin_t": c(sin.astype(np.float32)),
        "hadamard": hadamard_matrix(P), "identity": np.eye(P, dtype=np.float32), "causal": causal,
    }
    nc = bacc.Bacc("TRN2", target_bir_lowering=False, num_devices=1)
    args = [nc.dram_tensor(k, v.shape, mybir.dt.from_np(v.dtype), kind="ExternalInput").ap() for k, v in arrays.items()]
    out = nc.dram_tensor("out", (TOK, D), F32, kind="ExternalOutput").ap()
    build_program(nc, *args, out)
    r = run_bass_kernel_spmd(nc, [arrays], core_ids=[0])
    return r.results[0]["out"].reshape(B, S, D)
```
